# Optimizing a Trainium2 kernel written in Bass

```python
import numpy as np
import jax
import jax.numpy as jnp

def _softmax(x, axis=-1):
    return jax.nn.softmax(x, axis=axis)

def _gelu(x):
    return jax.nn.gelu(x, approximate=True)

def _silu(x):
    return jax.nn.silu(x)

def _sigmoid(x):
    return jax.nn.sigmoid(x)

def _layernorm(x, axis=-1, eps=1e-05):
    m = jnp.mean(x, axis=axis, keepdims=True)
    v = jnp.var(x, axis=axis, keepdims=True)
    return (x - m) / jnp.sqrt(v + eps)

def _scatter_add(tgt, idx, src, axis=0):
    return tgt.at[idx].add(src)

def _segment_sum(src, seg, n):
    return jax.ops.segment_sum(src, seg, n)
kernel_name = 'mk_gnn_resnorm_d4_gnn_r8_82eff2'

def setup_inputs(seed: int=0):
    np.random.seed(seed)
    _w = jnp.asarray

    def _rec_inputs():
        import jax
        import jax.numpy as jnp
        _gk = jax.random.key(seed)
        x = -0.0003713 + 1 * jax.random.normal(jax.random.fold_in(_gk, 1), (6250, 128), jnp.float32)
        _s = jax.random.randint(jax.random.fold_in(_gk, 2), (50000,), 0, 6250, jnp.int32)
        _d = jax.random.randint(jax.random.fold_in(_gk, 3), (50000,), 0, 6250, jnp.int32)
        _loop = jnp.arange(6250, dtype=jnp.int32)
        src = jnp.concatenate([_s, _d, _loop])
        dst = jnp.concatenate([_d, _s, _loop])
        _o = jnp.argsort(dst, stable=True)
        src = src[_o]
        dst = dst[_o]
        edge_type_64 = jax.random.randint(jax.random.fold_in(_gk, 13), (106250,), 0, 64, jnp.int32)
        edge_type_8 = jax.random.randint(jax.random.fold_in(_gk, 14), (106250,), 0, 8, jnp.int32)
        return (x, src, dst, edge_type_64, edge_type_8)
    x, src, dst, edge_type_64, edge_type_8 = _rec_inputs()

    def _L0_gnn_setup():
        import jax, jax.numpy as jnp
        import numpy as np
        N_NODES = 12500
        N_EDGES = 125000
        IN_DIM = 128
        OUT_DIM = 128
        N_REL = 64
        key = jax.random.key(seed)
        ks = jax.random.split(key, 7)
        s = 1.0 / np.sqrt(IN_DIM)
        return {'x': jax.random.normal(ks[0], (N_NODES, IN_DIM), dtype=jnp.float32), 'edge_index': jax.random.randint(ks[1], (2, N_EDGES), 0, N_NODES, dtype=jnp.int64), 'edge_type': jax.random.randint(ks[2], (N_EDGES,), 0, N_REL, dtype=jnp.int64), 'W': jax.random.normal(ks[3], (IN_DIM, OUT_DIM), dtype=jnp.float32) * s, 'W_r': jax.random.normal(ks[4], (IN_DIM, OUT_DIM), dtype=jnp.float32) * s, 'a': jax.random.normal(ks[5], (3 * OUT_DIM,), dtype=jnp.float32) * (1.0 / np.sqrt(3 * OUT_DIM)), 'rel_emb': jax.random.normal(ks[6], (N_REL, IN_DIM), dtype=jnp.float32) * s}
    _L0_gnn_all = _L0_gnn_setup()
    _L0_gnn_in = {k: v for k, v in _L0_gnn_all.items() if k in ('W', 'W_r', 'a', 'rel_emb')}
    del _L0_gnn_all

    def _L1_gnn_setup():
        import jax, jax.numpy as jnp
        import numpy as np
        N_NODES = 6250
        N_EDGES = 75000
        D_IN = 128
        D_HID = 128
        D_OUT = 128

        def _gin_conv(h, src, dst, n_nodes, Wa, ba, Wb, bb):
            agg = jax.ops.segment_sum(h[src], dst, num_segments=n_nodes)
            z = h + agg
            z = jax.nn.relu(z @ Wa + ba)
            return z @ Wb + bb
        key = jax.random.key(seed)
        ks = jax.random.split(key, 10)
        x = jax.random.normal(ks[0], (N_NODES, D_IN), dtype=jnp.float32)
        edge_index = jax.random.randint(ks[1], (2, N_EDGES), 0, N_NODES, dtype=jnp.int64)
        s = 1.0 / np.sqrt(D_IN)
        W1a = jax.random.uniform(ks[2], (D_IN, D_HID), jnp.float32, -s, s)
        b1a = jax.random.uniform(ks[3], (D_HID,), jnp.float32, -s, s)
        sh = 1.0 / np.sqrt(D_HID)
        W1b = jax.random.uniform(ks[4], (D_HID, D_HID), jnp.float32, -sh, sh)
        b1b = jax.random.uniform(ks[5], (D_HID,), jnp.float32, -sh, sh)
        W2a = jax.random.uniform(ks[6], (D_HID, D_HID), jnp.float32, -sh, sh)
        b2a = jax.random.uniform(ks[7], (D_HID,), jnp.float32, -sh, sh)
        W2b = jax.random.uniform(ks[8], (D_HID, D_OUT), jnp.float32, -sh, sh)
        b2b = jax.random.uniform(ks[9], (D_OUT,), jnp.float32, -sh, sh)
        return {'x': x, 'edge_index': edge_index, 'W1a': W1a, 'b1a': b1a, 'W1b': W1b, 'b1b': b1b, 'W2a': W2a, 'b2a': b2a, 'W2b': W2b, 'b2b': b2b}
    _L1_gnn_all = _L1_gnn_setup()
    _L1_gnn_in = {k: v for k, v in _L1_gnn_all.items() if k in ('W1a', 'b1a', 'W1b', 'b1b', 'W2a', 'b2a', 'W2b', 'b2b')}
    del _L1_gnn_all

    def _L2_gnn_setup():
        import jax, jax.numpy as jnp
        import numpy as np
        NUM_NODES = 6250
        NUM_EDGES = 200000
        DIM = 128
        NUM_REL = 8
        NUM_LAYERS = 2

        def _rgcn_conv(x, W, root, bias, src, dst, etype):
            R, N = (W.shape[0], x.shape[0])
            xW = jnp.einsum('ni,rio->rno', x, W)
            msgs = xW[etype, src]
            seg = etype * N + dst
            agg = jax.ops.segment_sum(msgs, seg, num_segments=R * N)
            cnt = jax.ops.segment_sum(jnp.ones_like(seg, dtype=x.dtype), seg, num_segments=R * N)
            agg = agg / jnp.maximum(cnt, 1.0)[:, None]
            agg = agg.reshape(R, N, -1).sum(axis=0)
            return agg + x @ root + bias
        key = jax.random.key(seed)
        ks = jax.random.split(key, 8)
        x = jax.random.normal(ks[0], (NUM_NODES, DIM), dtype=jnp.float32)
        edge_index = jax.random.randint(ks[1], (2, NUM_EDGES), 0, NUM_NODES, dtype=jnp.int32)
        edge_types = jax.random.randint(ks[2], (NUM_EDGES,), 0, NUM_REL, dtype=jnp.int32)
        scale = 1.0 / np.sqrt(DIM)
        weights = jax.random.normal(ks[3], (NUM_LAYERS, NUM_REL, DIM, DIM), dtype=jnp.float32) * scale
        roots = jax.random.normal(ks[4], (NUM_LAYERS, DIM, DIM), dtype=jnp.float32) * scale
        biases = jnp.zeros((NUM_LAYERS, DIM), dtype=jnp.float32)
        return {'x': x, 'weights': weights, 'roots': roots, 'biases': biases, 'edge_index': edge_index, 'edge_types': edge_types}
    _L2_gnn_all = _L2_gnn_setup()
    _L2_gnn_in = {k: v for k, v in _L2_gnn_all.items() if k in ('weights', 'roots', 'biases')}
    del _L2_gnn_all

    def _L3_gnn_setup():
        import jax, jax.numpy as jnp
        import numpy as np
        N_NODES = 12500
        N_EDGES = 200000
        IN_FEAT = 128
        OUT_FEAT = 128
        NUM_RELS = 8
        NUM_BASES = 2
        key = jax.random.key(seed)
        ks = jax.random.split(key, 8)
        feat = jax.random.normal(ks[0], (N_NODES, IN_FEAT), dtype=jnp.float32)
        edge_src = jax.random.randint(ks[1], (N_EDGES,), 0, N_NODES, dtype=jnp.int32)
        edge_dst = jnp.sort(jax.random.randint(ks[2], (N_EDGES,), 0, N_NODES, dtype=jnp.int32))
        etypes = jax.random.randint(ks[3], (N_EDGES,), 0, NUM_RELS, dtype=jnp.int32)
        bound = 1.0 / np.sqrt(IN_FEAT)
        W = jax.random.uniform(ks[4], (NUM_BASES + 1, IN_FEAT, OUT_FEAT), dtype=jnp.float32, minval=-bound, maxval=bound)
        coeff = jax.random.normal(ks[5], (NUM_RELS, NUM_BASES), dtype=jnp.float32) * np.sqrt(2.0 / (NUM_RELS + NUM_BASES))
        h_bias = jnp.zeros((OUT_FEAT,), dtype=jnp.float32)
        loop_weight = jax.random.normal(ks[6], (IN_FEAT, OUT_FEAT), dtype=jnp.float32) * np.sqrt(2.0 / (IN_FEAT + OUT_FEAT))
        return {'feat': feat, 'coeff': coeff, 'W': W, 'h_bias': h_bias, 'loop_weight': loop_weight, 'edge_src': edge_src, 'edge_dst': edge_dst, 'etypes': etypes}
    _L3_gnn_all = _L3_gnn_setup()
    _L3_gnn_in = {k: v for k, v in _L3_gnn_all.items() if k in ('coeff', 'W', 'h_bias', 'loop_weight')}
    del _L3_gnn_all
    return {'x': x, 'src': src, 'dst': dst, 'edge_type_64': edge_type_64, 'edge_type_8': edge_type_8, 'L0_gnn_W': _L0_gnn_in['W'], 'L0_gnn_W_r': _L0_gnn_in['W_r'], 'L0_gnn_a': _L0_gnn_in['a'], 'L0_gnn_rel_emb': _L0_gnn_in['rel_emb'], 'L1_gnn_W1a': _L1_gnn_in['W1a'], 'L1_gnn_b1a': _L1_gnn_in['b1a'], 'L1_gnn_W1b': _L1_gnn_in['W1b'], 'L1_gnn_b1b': _L1_gnn_in['b1b'], 'L1_gnn_W2a': _L1_gnn_in['W2a'], 'L1_gnn_b2a': _L1_gnn_in['b2a'], 'L1_gnn_W2b': _L1_gnn_in['W2b'], 'L1_gnn_b2b': _L1_gnn_in['b2b'], 'L2_gnn_weights': _L2_gnn_in['weights'], 'L2_gnn_roots': _L2_gnn_in['roots'], 'L2_gnn_biases': _L2_gnn_in['biases'], 'L3_gnn_coeff': _L3_gnn_in['coeff'], 'L3_gnn_W': _L3_gnn_in['W'], 'L3_gnn_h_bias': _L3_gnn_in['h_bias'], 'L3_gnn_loop_weight': _L3_gnn_in['loop_weight']}

def reference(x, src, dst, edge_type_64, edge_type_8, L0_gnn_W, L0_gnn_W_r, L0_gnn_a, L0_gnn_rel_emb, L1_gnn_W1a, L1_gnn_b1a, L1_gnn_W1b, L1_gnn_b1b, L1_gnn_W2a, L1_gnn_b2a, L1_gnn_W2b, L1_gnn_b2b, L2_gnn_weights, L2_gnn_roots, L2_gnn_biases, L3_gnn_coeff, L3_gnn_W, L3_gnn_h_bias, L3_gnn_loop_weight):
    import jax
    import jax.numpy as jnp

    def _L0_gnn_ref(x, edge_index, edge_type, W, W_r, a, rel_emb):
        import jax, jax.numpy as jnp
        import numpy as np
        N_NODES = 12500
        N_EDGES = 125000
        IN_DIM = 128
        OUT_DIM = 128
        N_REL = 64
        src, dst = (edge_index[0], edge_index[1])
        n = x.shape[0]
        xt = x @ W
        r = rel_emb[edge_type] @ W_r
        a1, a2, a3 = jnp.split(a, 3)
        att = jax.nn.leaky_relu(xt[src] @ a1 + r @ a2 + xt[dst] @ a3, negative_slope=0.2)
        att = att - att.max()
        att_exp = jnp.exp(att)
        att_sum = jax.ops.segment_sum(att_exp, dst, num_segments=n)
        att_norm = att_exp / (att_sum[dst] + 1e-10)
        msg = att_norm[:, None] * xt[src]
        out = jax.ops.segment_sum(msg, dst, num_segments=n)
        return out

    def _L1_gnn_ref(x, edge_index, W1a, b1a, W1b, b1b, W2a, b2a, W2b, b2b):
        import jax, jax.numpy as jnp
        import numpy as np
        N_NODES = 6250
        N_EDGES = 75000
        D_IN = 128
        D_HID = 128
        D_OUT = 128

        def _gin_conv(h, src, dst, n_nodes, Wa, ba, Wb, bb):
            agg = jax.ops.segment_sum(h[src], dst, num_segments=n_nodes)
            z = h + agg
            z = jax.nn.relu(z @ Wa + ba)
            return z @ Wb + bb
        src, dst = (edge_index[0], edge_index[1])
        n = x.shape[0]
        h = jax.nn.relu(_gin_conv(x, src, dst, n, W1a, b1a, W1b, b1b))
        out = _gin_conv(h, src, dst, n, W2a, b2a, W2b, b2b)
        return out

    def _L2_gnn_ref(x, weights, roots, biases, edge_index, edge_types):
        import jax, jax.numpy as jnp
        import numpy as np
        NUM_NODES = 6250
        NUM_EDGES = 200000
        DIM = 128
        NUM_REL = 8
        NUM_LAYERS = 2

        def _rgcn_conv(x, W, root, bias, src, dst, etype):
            R, N = (W.shape[0], x.shape[0])
            xW = jnp.einsum('ni,rio->rno', x, W)
            msgs = xW[etype, src]
            seg = etype * N + dst
            agg = jax.ops.segment_sum(msgs, seg, num_segments=R * N)
            cnt = jax.ops.segment_sum(jnp.ones_like(seg, dtype=x.dtype), seg, num_segments=R * N)
            agg = agg / jnp.maximum(cnt, 1.0)[:, None]
            agg = agg.reshape(R, N, -1).sum(axis=0)
            return agg + x @ root + bias
        src, dst = (edge_index[0], edge_index[1])
        h = x
        for l in range(NUM_LAYERS - 1):
            h = _rgcn_conv(h, weights[l], roots[l], biases[l], src, dst, edge_types)
            h = jax.nn.relu(h)
        h = _rgcn_conv(h, weights[-1], roots[-1], biases[-1], src, dst, edge_types)
        return h

    def _L3_gnn_ref(feat, coeff, W, h_bias, loop_weight, edge_src, edge_dst, etypes):
        import jax, jax.numpy as jnp
        import numpy as np
        N_NODES = 12500
        N_EDGES = 200000
        IN_FEAT = 128
        OUT_FEAT = 128
        NUM_RELS = 8
        NUM_BASES = 2
        n_dst = feat.shape[0]
        n_bases = coeff.shape[-1]
        msg = feat[edge_src]
        w = coeff[etypes]
        blocks = [feat[:n_dst]]
        for b in range(n_bases):
            blocks.append(jax.ops.segment_sum(w[:, b:b + 1] * msg, edge_dst, num_segments=n_dst))
        agg_out = jnp.concatenate(blocks, axis=-1)
        out = agg_out @ W.reshape(-1, W.shape[-1])
        h = out + h_bias + feat[:n_dst] @ loop_weight
        return h
    edge_index = jnp.stack([src, dst])
    x = _layernorm(x + _L0_gnn_ref(x, edge_index, edge_type_64, L0_gnn_W, L0_gnn_W_r, L0_gnn_a, L0_gnn_rel_emb), axis=-1)
    x = _layernorm(x + _L1_gnn_ref(x, edge_index, L1_gnn_W1a, L1_gnn_b1a, L1_gnn_W1b, L1_gnn_b1b, L1_gnn_W2a, L1_gnn_b2a, L1_gnn_W2b, L1_gnn_b2b), axis=-1)
    x = _layernorm(x + _L2_gnn_ref(x, L2_gnn_weights, L2_gnn_roots, L2_gnn_biases, edge_index, edge_type_8), axis=-1)
    x = _layernorm(x + _L3_gnn_ref(x, L3_gnn_coeff, L3_gnn_W, L3_gnn_h_bias, L3_gnn_loop_weight, src, dst, edge_type_8), axis=-1)
    return x

_drawn_inputs = setup_inputs


def setup_inputs(seed=0):
    import zlib

    import numpy as np

    out = dict(_drawn_inputs(seed))
    spreads = {'L2_gnn_biases': (0.0, 0.1), 'L3_gnn_h_bias': (0.0, 0.1)}
    factors = {'L0_gnn_W_r': 8.0, 'L0_gnn_rel_emb': 8.0, 'L1_gnn_b1a': 4.083, 'L1_gnn_b2a': 8.0}
    for name, (base, spread) in spreads.items():
        noise = np.random.default_rng([zlib.crc32(name.encode()), seed]).standard_normal(out[name].shape)
        drawn = base * np.exp(spread * noise) if base else spread * noise
        out[name] = jnp.asarray(drawn.astype(out[name].dtype))
    for name, factor in factors.items():
        out[name] = (out[name] * factor).astype(out[name].dtype)
    return out
```

```python
import numpy as np
import concourse.bass as bass
from concourse import mybir

F32 = mybir.dt.float32
I32 = mybir.dt.int32
ALU = mybir.AluOpType
ACT = mybir.ActivationFunctionType
AX = mybir.AxisListType

P = 128
D = 128
W = 64
QUAD = 4
G = 16
GQ = G // QUAD
TURN = 7 * P
HALF = (512, TURN - 512)
HOFF = (0, 512)
NREL = 8
BIG = 1.0e30
LOWEST = -3.0e38


def round_up(a, b):
    return (a + b - 1) // b * b


def sizes(n_nodes, n_edges):
    return round_up(n_nodes, TURN), round_up(-(-n_edges // P), 2 * G)


MATS = ["W", "W1a", "W1b", "W2a", "W2b", "root0", "root1", "V0", "V1", "V2", "loop", "WT", "WrT"]
BIAS = ["b1a", "b1b", "b2a", "b2b", "bias0", "bias1", "h_bias"]

GAT, GIN1, GIN2, RGCN1, RGCN2, BASIS = range(6)
FRONT = {
    GAT: (["guard", "recip", "norm", "sum"], [], ["lin"]),
    GIN1: (["zin", "keep"], ["hidden", "outr"], ["lin", "lin2"]),
    GIN2: (["zin", "sum"], ["hidden"], ["lin", "lin2"]),
    RGCN1: (["sum", "keep"], ["outr"], ["lin"]),
    RGCN2: (["sum0", "sum"], [], ["lin"]),
    BASIS: (["sum"], [], ["lin"]),
}
NORMED = (GAT, GIN2, RGCN2, BASIS)
ROWS = (GAT, GIN1, RGCN2)
WIDE = (GIN2, RGCN1)


def steps_of(p):
    v, a, t = (list(x) for x in FRONT[p])
    if p in NORMED:
        v += ["center", "rstd", "out"]
        a += ["square", "std", "store"]
        t += ["mean", "var"]
    return v, a, t


def build(nc, N, E, x_rows, xT, src_pt, dst_pt, dst_q, et64_pt, et8_pt, et8_flat, mats, bias, avec, relT, tw0, tw1,
          coeff, outT):
    NP, NCH = sizes(N, E)
    NQ = NCH // QUAD
    QP = NQ // 2
    NB = NCH // (2 * G)
    NT = NP // TURN
    NSW = NP // W
    from contextlib import ExitStack
    ctx = ExitStack()
    with ctx:
        def sb(name, shape, dt=F32):
            return ctx.enter_context(nc.sbuf_tensor(name, shape, dt))

        def sem(name):
            return ctx.enter_context(nc.semaphore(name))

        def dram(name, shape, dt=F32):
            return nc.dram_tensor(name, shape, dt, kind="Internal").ap()

        table0 = dram("table0", [NP, D + 1])
        table_gin1 = dram("table_gin1", [NP, D])
        table_gin2 = dram("table_gin2", [NP, D])
        table_rel1 = dram("table_rel1", [NP * NREL, D])
        table_rel2 = dram("table_rel2", [NP * NREL, D])
        table_basis = dram("table_basis", [NP, D])
        base_d = dram("base_d", [1, NQ])
        wide_d = dram("wide_d", [1, QP])
        tables = {GAT: table0, GIN1: table_gin1, GIN2: table_gin2, RGCN1: table_rel1, RGCN2: table_rel2,
                  BASIS: table_basis}
        next_table = {GAT: table_gin1, GIN1: table_gin2, GIN2: table_rel1, RGCN1: table_rel2, RGCN2: table_basis}

        acc = sb("acc", [P, 2, NP])
        X = sb("X", [P, NP])
        H = sb("H", [P, NP])
        msgs = [sb(f"msgs{k}", [P, G, D + 1]) for k in range(2)]
        wo = [sb(f"wo{k}", [P, G, 2, W]) for k in range(2)]
        idx = [sb(f"idx{k}", [P, G], I32) for k in range(2)]
        work = sb("work", [P, 6 * TURN])
        src_i = sb("src_i", [P, NCH], I32)
        row_i = sb("row_i", [P, NCH], I32)
        dst_i = sb("dst_i", [P, NCH], I32)
        et64_i = sb("et64_i", [P, NCH], I32)
        et8_i = sb("et8_i", [P, NCH], I32)
        rel = sb("rel", [P, NCH])
        neg = sb("neg", [P, NCH])
        w_edge = sb("w_edge", [P, NCH])
        w_edge2 = sb("w_edge2", [P, NCH])
        base_keep = sb("base_keep", [P, NQ])
        base_f = sb("base_f", [P, NQ])
        base_i = sb("base_i", [1, NQ], I32)
        wide = sb("wide", [P, QP])
        flag = sb("flag", [P, 4])
        sweeps_f = sb("sweeps_f", [1, 1])
        sweeps_i = sb("sweeps_i", [1, 1], I32)
        bq = sb("bq", [QP, 2])
        mq = sb("mq", [QP, 2])
        wq = sb("wq", [QP, 1])
        m_sb = sb("m_sb", [P, len(MATS), D])
        b_sb = sb("b_sb", [P, len(BIAS)])
        a_sb = sb("a_sb", [P, 3])
        relT_sb = sb("relT_sb", [P, 64])
        tw = sb("tw", [P, NREL * D])
        coef = sb("coef", [P, NREL * 2])
        vv = sb("vv", [P, 3])
        v3b = sb("v3b", [P, P])
        u2b = sb("u2b", [P, P])
        c64 = sb("c64", [P, 64])
        pcol = sb("pcol", [P, NP // P])
        iota_i = sb("iota_i", [P, P], I32)
        iota = sb("iota", [P, P])
        pidx_i = sb("pidx_i", [P, 1], I32)
        pidx = sb("pidx", [P, 1])
        ident = sb("ident", [P, P])
        ones = sb("ones", [P, P])
        mean_m = sb("mean_m", [P, P])
        oe = [sb(f"oe{k}", [P, G, NREL]) for k in range(2)]
        s_q = sb("s_q", [P, G])
        s_c = sb("s_c", [P, G])
        att = sb("att", [P, 2, G])
        ex = sb("ex", [P, 2, G])
        gm = sb("gm", [P, 2])
        gx = sb("gx", [1, 2])
        Rmax = sb("Rmax", [P, 2])
        dR = sb("dR", [P, 2])
        nR = sb("nR", [P, 2])
        alpha = sb("alpha", [P, 2])
        rows_sb = [sb(f"rows_sb{h}", [P, HALF[h]]) for h in range(2)]
        eps = sb("eps", [P, 1])

        oh = work[:, 0:G * W].rearrange("p (g w) -> p g w", g=G)
        tmp = work[:, G * W:2 * G * W].rearrange("p (g w) -> p g w", g=G)
        tmp2 = work[:, 2 * G * W:3 * G * W].rearrange("p (g w) -> p g w", g=G)
        et_b = work[0:NREL, 3 * G * W:3 * G * W + G * P]

        def part(k, h):
            return work[:, k * TURN + HOFF[h]:k * TURN + HOFF[h] + HALF[h]]
        wide_rows = [acc[:, 1, k * NREL * D:(k + 1) * NREL * D] for k in range(min(4, NP // (NREL * D)))]
        if len(wide_rows) < 4:
            wide_rows = [sb(f"wide_rows{k}", [P, NREL * D])[:, :] for k in range(4)]

        bank = [ctx.enter_context(nc.psum_tensor(f"bank{k}", [P, 512], F32)) for k in range(8)]

        def mat(name):
            return m_sb[:, MATS.index(name), :]

        def bcol(name):
            k = BIAS.index(name)
            return b_sb[:, k:k + 1]

        loaded = sem("loaded")
        gathering = sem("gathering")
        x_copied = sem("x_copied")
        pcol_out = sem("pcol_out")
        consts = sem("consts")
        v0 = sem("v0")
        a0 = sem("a0")
        t0 = sem("t0")
        based = sem("based")
        based_back = sem("based_back")
        S = [dict() for _ in range(6)]
        for p in range(6):
            for k in range(2):
                for n in ("idx_ready", "landed", "weights_ready", "chunk_done", "taken"):
                    S[p][n, k] = sem(f"{n}{k}_{p}")
                if p in ROWS:
                    for n in ("rows_ready", "rows_copied", "rows_stored"):
                        S[p][n, k] = sem(f"{n}{k}_{p}")
            for n in ("setup", "chain", "vn", "an", "tn"):
                S[p][n] = sem(f"{n}_{p}")
            if p in WIDE:
                for n in ("lo_ready", "hi_ready", "lo_taken", "hi_taken"):
                    S[p][n] = sem(f"{n}_{p}")
                for k in range(4):
                    S[p]["wide_stored", k] = sem(f"wide_stored{k}_{p}")
        gmax_part, gmax_t, gmax_row, gmax_all, shift_ready, exp_ready = (
            sem(n) for n in ("gmax_part", "gmax_t", "gmax_row", "gmax_all", "shift_ready", "exp_ready"))
        rescaled = [sem(f"rescaled{k}") for k in range(2)]
        types_loaded, types_hot, picked = (sem(n) for n in ("types_loaded", "types_hot", "picked"))
        tw_loaded = sem("tw_loaded")
        out_stored = [sem(f"out_stored{h}") for h in range(2)]

        NLOAD = 13
        block = ctx.enter_context(nc.Block())

        def sweeps(eng):
            eng.wait_ge(v0, V0["sweeps"])
            return eng.value_load(sweeps_i[0:1, 0:1], min_val=1, max_val=NSW)

        def n_steps(p, e):
            return 2 * len(steps_of(p)[e])

        def step_at(p, e, name, h):
            return 2 * steps_of(p)[e].index(name) + h + 1

        V0 = {n: k + 1 for k, n in enumerate(
            ["iota", "pidx", "ident", "ones", "mean", "qmin", "qcl", "qmsk", "qmax", "qspan", "qwide", "vv", "v3b", "u2b",
             "c64", "pcol", "row8", "row", "flag", "wflag", "keepf", "base_keep", "sw0", "sweeps_f", "sweeps", "R",
             "eps"])}
        T0 = {n: k + 1 for k, n in enumerate(["vv", "c64", "pcol"])}
        TQ = len(T0)
        SETUP = {p: (8 if p == GAT else 4) for p in range(6)}
        CHAIN = {GAT: 2 * (14 + GQ - 1), GIN1: 2 * (1 + 2 * GQ - 1), GIN2: 2 * (4 + GQ - 1), RGCN1: 2 * (1 + GQ - 1),
                 RGCN2: 2 * (1 + GQ - 1), BASIS: 2 * (2 + GQ - 1)}
        PRE = {GAT: 1, GIN1: 2, GIN2: 4, RGCN1: 1, RGCN2: 1, BASIS: 1 + 4 * NREL}

        @block.sync
        def _(sp):
            for dst, src in ((X[:], xT), (src_i[:], src_pt), (dst_i[:], dst_pt), (et64_i[:], et64_pt),
                             (et8_i[:], et8_pt), (m_sb[:], mats.rearrange("p (k d) -> p k d", d=D)), (b_sb[:], bias),
                             (a_sb[:], avec), (relT_sb[:], relT), (tw[:], tw0),
                             (coef[:], coeff.to_broadcast([P, NREL * 2])),
                             (work[0:QP, 0:2 * QUAD * P].bitcast(I32), dst_q)):
                sp.dma_start(dst, src).then_inc(loaded, 16)
            sp.dma_start(work[0:1, 3 * TURN:3 * TURN + 16], mats[0:1, 0:16]).then_inc(loaded, 16)
            sp.wait_ge(v0, V0["qwide"])
            sp.dma_start(base_d.rearrange("o (p k) -> (o p) k", k=2), bq[:]).then_inc(based, 16)
            sp.dma_start(wide_d.rearrange("o p -> p o"), wq[:]).then_inc(based, 16)
            sp.wait_ge(based, 32)
            sp.dma_start(base_keep[:], base_d.to_broadcast([P, NQ])).then_inc(based_back, 16)
            sp.dma_start(wide[:], wide_d.to_broadcast([P, QP])).then_inc(based_back, 16)
            sp.wait_ge(v0, V0["pcol"])
            sp.dma_start(table0.rearrange("(t p) c -> p t c", p=P)[:, :, D:D + 1],
                         pcol[:].unsqueeze(2)).then_inc(pcol_out, 16)
            ns = sweeps(sp)
            for p in range(6):
                s = S[p]
                if p == GIN2:
                    sp.wait_ge(S[GIN1]["vn"], n_steps(GIN1, 0) * NT)
                rows = row_i if p in (RGCN1, RGCN2) else src_i
                with sp.Fori(0, ns) as sw:
                    with sp.Fori(0, NB) as i:
                        t = sp.snap(sw * NB + i)
                        for k in range(2):
                            sp.wait_ge(s["landed", k], t * (16 * G))
                            sp.dma_start(idx[k][:], rows[:, bass.ds(i * (2 * G) + k * G, G)]).then_inc(s["idx_ready", k], 16)
                            if p == GIN2:
                                sp.wait_ge(picked, t * 2 + k)
                                sp.dma_start(et_b.bitcast(I32),
                                             et8_flat[0:1, bass.ds(i * (2 * G * P) + k * G * P, G * P)].to_broadcast(
                                                 [NREL, G * P])).then_inc(types_loaded, 16)
                with sp.Fori(0, NT) as i:
                    if p in ROWS:
                        view = next_table[p].rearrange("(t p) c -> p t c", p=P)
                        for h in range(2):
                            n = HALF[h] // P
                            sp.wait_ge(s["rows_copied", h], i + 1)
                            sp.dma_start(view[:, bass.ds(i * 7 + 4 * h, n), :],
                                         rows_sb[h][:].rearrange("p (t c) -> p t c", c=D)).then_inc(s["rows_stored", h], 16)
                    if p in WIDE:
                        view = next_table[p].rearrange("(t p r) c -> p t (r c)", p=P, r=NREL)
                        for k in range(7):
                            sp.wait_ge(s["lo_taken"], i * 7 + (k + 1))
                            sp.wait_ge(s["hi_taken"], i * 7 + (k + 1))
                            sp.dma_start(view[:, bass.ds(i * 7 + k, 1), :],
                                         wide_rows[k % 4].unsqueeze(1)).then_inc(s["wide_stored", k % 4], 16)
                    if p == BASIS:
                        for h in range(2):
                            sp.wait_ge(s["vn"], i * n_steps(p, 0) + step_at(p, 0, "out", h))
                            sp.dma_start(outT[:, bass.ds(i * TURN + HOFF[h], HALF[h])], part(5, h)).then_inc(out_stored[h], 16)
                if p == GIN2:
                    sp.wait_ge(s["hi_ready"], 7 * NT)
                    sp.dma_start(tw[:], tw1).then_inc(tw_loaded, 16)
            for h in range(2):
                sp.wait_ge(out_stored[h], 16 * NT)

        @block.gpsimd
        def _(pool):
            pool.dma_start(table0[:, 0:D], x_rows).then_inc(x_copied, 16)
            pool.iota(iota_i[:], pattern=[[1, P]], base=0, channel_multiplier=0).then_inc(consts, 1)
            pool.iota(pidx_i[:], pattern=[[0, 1]], base=0, channel_multiplier=1).then_inc(consts, 1)
            pool.wait_ge(x_copied, 16)
            pool.wait_ge(pcol_out, 16)
            ns = sweeps(pool)
            for p in range(6):
                s = S[p]
                if p and p - 1 in ROWS:
                    for h in range(2):
                        pool.wait_ge(S[p - 1]["rows_stored", h], 16 * NT)
                if p and p - 1 in WIDE:
                    for k in range(4):
                        pool.wait_ge(S[p - 1]["wide_stored", k], 16 * NT * len(range(k, 7, 4)))
                width = D + 1 if p == GAT else D
                with pool.Fori(0, ns) as sw:
                    with pool.Fori(0, NB) as i:
                        t = pool.snap(sw * NB + i)
                        for k in range(2):
                            pool.wait_ge(s["idx_ready", k], t * 16 + 16)
                            pool.wait_ge(s["chunk_done", k], t)
                            pool.sem_inc(gathering, 1)
                            for c in range(G):
                                pool.indirect_dma_start(
                                    out=msgs[k][:, c, 0:width], out_offset=None, in_=tables[p],
                                    in_offset=bass.IndirectOffsetOnAxis(ap=idx[k][:, c:c + 1], axis=0)).then_inc(s["landed", k], 16)

        @block.scalar
        def _(act):
            with act.Fori(0, NT) as i:
                for h in range(2):
                    act.wait_ge(t0, i * 2 + (TQ + h + 1))
                    nc.scalar.activation(H[:, bass.ds(i * TURN + HOFF[h], HALF[h])], bank[2 + h][:, 0:HALF[h]],
                                         ACT.Copy).then_inc(a0, 1)
            ns = sweeps(act)
            for p in range(6):
                s = S[p]
                v, a, tt = s["vn"], s["an"], s["tn"]
                KV, KA, KT = (n_steps(p, e) for e in range(3))
                if p == GAT:
                    with act.Fori(0, ns) as sw:
                        with act.Fori(0, NB) as i:
                            t = act.snap(sw * NB + i)
                            for k in range(2):
                                act.wait_ge(shift_ready, t * 4 + (2 * k + 2))
                                nc.scalar.activation(ex[:, k, :], att[:, k, :], ACT.Exp, bias=nR[:, k:k + 1]).then_inc(exp_ready, 1)
                                nc.scalar.activation(alpha[:, k:k + 1], dR[:, k:k + 1], ACT.Exp).then_inc(exp_ready, 1)
                                act.wait_ge(exp_ready, t * 4 + (2 * k + 2))
                                act.wait_ge(s["taken", 1 - k], t + k)
                                if k == 0:
                                    act.wait_ge(s["chain"], 1)
                                flat = acc[:].rearrange("p a n -> p (a n)")
                                nc.scalar.activation(flat, flat, ACT.Copy, scale=alpha[:, k:k + 1]).then_inc(rescaled[k], 1)
                with act.Fori(0, NT) as i:
                    va, aa, ta = act.snap(i * KV), act.snap(i * KA), act.snap(i * KT)

                    def after(sm, base, e, name, h):
                        act.wait_ge(sm, base + step_at(p, e, name, h))

                    def col(h):
                        return bass.ds(i * TURN + HOFF[h], HALF[h])
                    if p in (GIN1, GIN2):
                        for h in range(2):
                            after(tt, ta, 2, "lin", h)
                            nc.scalar.activation(part(1, h), bank[2 + h][:, 0:HALF[h]], ACT.Relu,
                                                 bias=bcol("b1a" if p == GIN1 else "b2a")).then_inc(a, 1)
                    if p == GIN1:
                        for h in range(2):
                            after(tt, ta, 2, "lin2", h)
                            act.wait_ge(v, va)
                            act.wait_ge(s["rows_ready", h], i)
                            nc.scalar.activation(part(5, h), bank[4 + h][:, 0:HALF[h]], ACT.Relu, bias=bcol("b1b")).then_inc(a, 1)
                    if p == RGCN1:
                        for h in range(2):
                            after(v, va, 0, "sum", h)
                            act.wait_ge(s["hi_ready"], i * 7)
                            nc.scalar.activation(part(5, h), part(2, h), ACT.Relu, bias=bcol("bias0")).then_inc(a, 1)
                    if p in NORMED:
                        for h in range(2):
                            after(v, va, 0, "center", h)
                            nc.scalar.activation(part(4, h), part(3, h), ACT.Square).then_inc(a, 1)
                        for h in range(2):
                            after(tt, ta, 2, "var", h)
                            nc.scalar.activation(part(1, h), bank[6 + h][:, 0:HALF[h]], ACT.Sqrt, bias=eps[:, 0:1]).then_inc(a, 1)
                        for h in range(2):
                            after(v, va, 0, "out", h)
                            nc.scalar.activation(X[:, col(h)], part(5, h), ACT.Copy).then_inc(a, 1)
                    if p in ROWS:
                        for h in range(2):
                            act.wait_ge(s["rows_ready", h], i + 1)
                            act.wait_ge(s["rows_stored", h], i * 16)
                            nc.scalar.activation(rows_sb[h][:], bank[h][:, 0:HALF[h]], ACT.Copy).then_inc(s["rows_copied", h], 1)
                    if p in WIDE:
                        for k in range(7):
                            act.wait_ge(s["lo_ready"], i * 7 + (k + 1))
                            act.wait_ge(s["wide_stored", k % 4], i * (16 * len(range(k % 4, 7, 4))) + 16 * (k // 4))
                            nc.scalar.activation(wide_rows[k % 4][:, 0:512], bank[0][:], ACT.Copy).then_inc(s["lo_taken"], 1)

        @block.tensor
        def _(pe):
            pe.wait_ge(loaded, 16 * NLOAD)
            pe.matmul(bank[0][:, 0:1], mat("WT"), a_sb[:, 0:1], start=True, stop=True)
            pe.matmul(bank[0][:, 1:2], mat("WrT"), a_sb[:, 1:2], start=True, stop=True)
            pe.matmul(bank[0][:, 2:3], mat("WT"), a_sb[:, 2:3], start=True, stop=True).then_inc(t0, 1)
            pe.wait_ge(v0, V0["u2b"])
            pe.matmul(bank[1][:, 0:64], u2b[:], relT_sb[:], start=True, stop=True).then_inc(t0, 1)
            for n in range(NP // P):
                m = pe.matmul(bank[4][:, n:n + 1], X[:, n * P:(n + 1) * P], vv[:, 0:1], start=True, stop=True)
            m.then_inc(t0, 1)
            with pe.Fori(0, NT) as i:
                for h in range(2):
                    pe.wait_ge(a0, i * 2)
                    pe.matmul(bank[2 + h][:, 0:HALF[h]], v3b[:], X[:, bass.ds(i * TURN + HOFF[h], HALF[h])],
                              start=True, stop=True).then_inc(t0, 1)
            ns = sweeps(pe)
            pe.wait_ge(a0, 2 * NT)
            for p in range(6):
                s = S[p]
                with pe.Fori(0, ns) as sw:
                    with pe.Fori(0, NB) as i:
                        t = pe.snap(sw * NB + i)
                        for k in range(2):
                            if p == GAT:
                                pe.wait_ge(gmax_part, t * 2 + (k + 1))
                                pe.matmul(bank[2][0:1, 0:P], gm[:, k:k + 1], ident[:], start=True, stop=True).then_inc(gmax_t, 1)
                                pe.wait_ge(gmax_row, t * 2 + (k + 1))
                                pe.matmul(bank[3][:, 0:1], ones[0:1, :], gx[0:1, k:k + 1], start=True, stop=True).then_inc(gmax_all, 1)
                            if p == GIN2:
                                pe.wait_ge(s["setup"], sw * SETUP[p] + SETUP[p])
                                pe.wait_ge(s["chain"], PRE[p])
                                first = [pe.value_load(base_i[0:1, bass.ds(i * (2 * GQ) + k * GQ + q, 1)], min_val=0,
                                                       max_val=NP - W) for q in range(GQ)]
                                pe.wait_ge(types_hot, t * 2 + (k + 1))
                                for c in range(G):
                                    m = pe.matmul(bank[4 + c // 8][:, (c % 8) * W:(c % 8 + 1) * W],
                                                  et_b[:, c * P:(c + 1) * P], acc[0:NREL, 1, bass.ds(first[c // QUAD], W)],
                                                  start=True, stop=True)
                                m.then_inc(picked, 1)
                            pe.wait_ge(s["weights_ready", k], t + 1)
                            pe.wait_ge(s["landed", k], t * (16 * G) + 16 * G)
                            pe.wait_ge(s["taken", k], t)
                            for q in range(GQ):
                                o = bank[k][:, q * 2 * W:(q + 1) * 2 * W]
                                for c in range(q * QUAD, (q + 1) * QUAD):
                                    st = dict(start=c % QUAD == 0, stop=c % QUAD == QUAD - 1)
                                    if p == BASIS:
                                        m = pe.matmul(o, msgs[k][:, c, 0:D], wo[k][:, c, :, :].rearrange("p a w -> p (a w)"), **st)
                                    else:
                                        m = pe.matmul(o[:, 0:W], msgs[k][:, c, 0:D], wo[k][:, c, 0, :], **st)
                                for c in range(q * QUAD, (q + 1) * QUAD):
                                    st = dict(start=c % QUAD == 0, stop=c % QUAD == QUAD - 1)
                                    if p == GAT:
                                        m = pe.matmul(o[:, W:2 * W], ones[:], wo[k][:, c, 0, :], **st)
                                    if p == GIN1:
                                        m = pe.matmul(o[0:NREL, W:2 * W], oe[k][:, c, :], wo[k][:, c, 0, :], **st)
                            m.then_inc(s["chunk_done", k], 1)
                v, a, tt = s["vn"], s["an"], s["tn"]
                KV, KA, KT = (n_steps(p, e) for e in range(3))
                if p == RGCN1:
                    pe.wait_ge(tw_loaded, 16)
                with pe.Fori(0, NT) as i:
                    va, aa, ta = pe.snap(i * KV), pe.snap(i * KA), pe.snap(i * KT)
                    for k in range(2):
                        pe.wait_ge(s["taken", k], ns * NB)

                    def after(sm, base, e, name, h):
                        pe.wait_ge(sm, base + step_at(p, e, name, h))

                    def col(h):
                        return bass.ds(i * TURN + HOFF[h], HALF[h])
                    pe.wait_ge(v, va)
                    pe.wait_ge(a, aa)
                    for h in range(2):
                        o = bank[2 + h][:, 0:HALF[h]]
                        if p == GAT:
                            after(v, va, 0, "norm", h)
                            pe.matmul(o, mat("W"), part(0, h), start=True, stop=True).then_inc(tt, 1)
                        if p in (GIN1, GIN2):
                            after(v, va, 0, "zin", h)
                            pe.matmul(o, mat("W1a" if p == GIN1 else "W2a"), part(0, h), start=True, stop=True).then_inc(tt, 1)
                        if p == RGCN1:
                            pe.matmul(o, mat("root0"), X[:, col(h)], start=True, stop=True).then_inc(tt, 1)
                        if p == RGCN2:
                            pe.matmul(o, mat("root1"), H[:, col(h)], start=True, stop=True).then_inc(tt, 1)
                        if p == BASIS:
                            pe.matmul(o, mat("V0"), X[:, col(h)], start=True, stop=False)
                            pe.matmul(o, mat("V1"), acc[:, 0, col(h)], start=False, stop=False)
                            pe.matmul(o, mat("V2"), acc[:, 1, col(h)], start=False, stop=False)
                            pe.matmul(o, mat("loop"), X[:, col(h)], start=False, stop=True).then_inc(tt, 1)
                    if p in (GIN1, GIN2):
                        for h in range(2):
                            after(a, aa, 1, "hidden", h)
                            pe.matmul(bank[4 + h][:, 0:HALF[h]], mat("W1b" if p == GIN1 else "W2b"), part(1, h),
                                      start=True, stop=True).then_inc(tt, 1)
                    if p in NORMED:
                        for h in range(2):
                            after(v, va, 0, "sum", h)
                            mb = 2 if p == GIN2 else 4
                            pe.matmul(bank[mb + h][:, 0:HALF[h]], mean_m[:], part(2, h), start=True, stop=True).then_inc(tt, 1)
                        for h in range(2):
                            after(a, aa, 1, "square", h)
                            pe.matmul(bank[6 + h][:, 0:HALF[h]], mean_m[:], part(4, h), start=True, stop=True).then_inc(tt, 1)

                    def after_out(h):
                        if p in NORMED:
                            after(v, va, 0, "out", h)
                        else:
                            after(a, aa, 1, "outr", h)
                    if p in ROWS:
                        for h in range(2):
                            after_out(h)
                            pe.wait_ge(s["rows_copied", h], i)
                            for k in range(HALF[h] // P):
                                m = pe.transpose(bank[h][:, k * P:(k + 1) * P], part(5, h)[:, k * P:(k + 1) * P], ident[:])
                            m.then_inc(s["rows_ready", h], 1)
                    if p in WIDE:
                        for k in range(7):
                            h = k // 4
                            if k in (0, 4):
                                after_out(h)
                            node = part(5, h)[:, (k - 4 * h) * P:(k - 4 * h + 1) * P]
                            pe.wait_ge(s["lo_taken"], i * 7 + k)
                            pe.matmul(bank[0][:], node, tw[:, 0:512], start=True, stop=True).then_inc(s["lo_ready"], 1)
                            pe.wait_ge(s["hi_taken"], i * 7 + k)
                            pe.matmul(bank[1][:], node, tw[:, 512:1024], start=True, stop=True).then_inc(s["hi_ready"], 1)
                if p in ROWS:
                    for h in range(2):
                        pe.wait_ge(s["rows_copied", h], NT)
                if p in WIDE:
                    pe.wait_ge(s["lo_taken"], 7 * NT)
                    pe.wait_ge(s["hi_taken"], 7 * NT)
                pe.wait_ge(v, KV * NT)
                pe.wait_ge(a, KA * NT)

        @block.vector
        def _(dve):
            vec = nc.vector

            def tick0(ins, name):
                ins.then_inc(v0, 1)
                dve.wait_ge(v0, V0[name])
            dve.wait_ge(consts, 2)
            tick0(vec.tensor_copy(iota[:], iota_i[:]), "iota")
            tick0(vec.tensor_copy(pidx[:], pidx_i[:]), "pidx")
            tick0(vec.tensor_scalar(ident[:], iota[:], pidx[:, 0:1], None, ALU.is_equal), "ident")
            tick0(vec.memset(ones[:], 1.0), "ones")
            tick0(vec.memset(mean_m[:], 1.0 / D), "mean")
            dve.wait_ge(loaded, 16 * NLOAD)
            dq = work[0:QP, 0:2 * QUAD * P].bitcast(I32).rearrange("p (k e) -> p k e", k=2)
            dm = work[0:QP, 2 * QUAD * P:4 * QUAD * P].rearrange("p (k e) -> p k e", k=2)
            tick0(vec.tensor_reduce(bq[:], dq, AX.X, ALU.min), "qmin")
            tick0(vec.tensor_scalar(bq[:], bq[:], float(NP - W), None, ALU.min), "qcl")
            tick0(vec.scalar_tensor_tensor(dm, dq, float(NP), dq, ALU.is_lt, ALU.mult), "qmsk")
            tick0(vec.tensor_reduce(mq[:], dm, AX.X, ALU.max), "qmax")
            tick0(vec.tensor_tensor(mq[:], mq[:], bq[:], ALU.subtract), "qspan")
            tick0(vec.tensor_reduce(wq[:], mq[:], AX.X, ALU.max), "qwide")
            dve.wait_ge(t0, T0["vv"])
            tick0(vec.tensor_copy(vv[:], bank[0][:, 0:3]), "vv")
            tick0(vec.tensor_scalar(v3b[:], ones[:], vv[:, 2:3], None, ALU.mult), "v3b")
            tick0(vec.tensor_scalar(u2b[:], ones[:], vv[:, 1:2], None, ALU.mult), "u2b")
            dve.wait_ge(t0, T0["c64"])
            tick0(vec.tensor_copy(c64[:], bank[1][:, 0:64]), "c64")
            dve.wait_ge(t0, T0["pcol"])
            tick0(vec.tensor_copy(pcol[:], bank[4][:, 0:NP // P]), "pcol")
            tick0(vec.tensor_scalar(row_i[:], src_i[:], float(NREL), None, ALU.mult), "row8")
            tick0(vec.tensor_tensor(row_i[:], row_i[:], et8_i[:], ALU.add), "row")
            dve.wait_ge(based_back, 32)
            wmax = s_q[:, 0:1]
            vec.tensor_reduce(wmax, wide[:], AX.X, ALU.max).then_inc(consts, 1)
            dve.wait_ge(consts, 3)
            tick0(vec.tensor_scalar(flag[:, 0:1], wmax, float(W), None, ALU.is_ge), "flag")
            tick0(vec.tensor_scalar(flag[:, 1:2], flag[:, 0:1], float(W), None, ALU.mult), "wflag")
            tick0(vec.tensor_scalar(flag[:, 2:3], flag[:, 0:1], -1.0, 1.0, ALU.mult, ALU.add), "keepf")
            tick0(vec.tensor_scalar(base_keep[:], base_keep[:], flag[:, 2:3], None, ALU.mult), "base_keep")
            tick0(vec.memset(flag[:, 3:4], 0.0), "sw0")
            tick0(vec.tensor_scalar(sweeps_f[:], flag[0:1, 0:1], float(NSW - 1), 1.0, ALU.mult, ALU.add), "sweeps_f")
            tick0(vec.tensor_copy(sweeps_i[:], sweeps_f[:]), "sweeps")
            tick0(vec.memset(Rmax[:], LOWEST), "R")
            tick0(vec.memset(eps[:], 1e-5), "eps")
            ns = sweeps(dve)
            dve.wait_ge(a0, 2 * NT)

            def over_w(ap):
                return ap.unsqueeze(2).broadcast_to([P, G, W])
            iota_w = iota[:, 0:W].unsqueeze(1).broadcast_to([P, G, W])
            for p in range(6):
                s = S[p]
                chain = s["chain"]
                n_pre = 0

                def pre(ins):
                    nonlocal n_pre
                    ins.then_inc(chain, 1)
                    n_pre += 1
                    dve.wait_ge(chain, n_pre)
                if p and p - 1 in WIDE and p != RGCN2:
                    for k in range(4):
                        dve.wait_ge(S[p - 1]["wide_stored", k], 16 * NT * len(range(k, 7, 4)))
                if p == BASIS:
                    for k in range(4):
                        dve.wait_ge(S[RGCN1]["wide_stored", k], 16 * NT * len(range(k, 7, 4)))
                if p in (GAT, BASIS):
                    pre(vec.memset(acc[:].rearrange("p a n -> p (a n)"), 0.0))
                elif p == GIN1:
                    pre(vec.memset(acc[:, 0, :], 0.0))
                    pre(vec.memset(acc[0:NREL, 1, :], 0.0))
                else:
                    pre(vec.memset(acc[:, 0, :], 0.0))
                if p == GIN2:
                    pre(vec.memset(w_edge[:], 0.0))
                    pre(vec.tensor_scalar(acc[0:NREL, 1, :], acc[0:NREL, 1, :], 1.0, None, ALU.max))
                    pre(vec.reciprocal(acc[0:NREL, 1, :], acc[0:NREL, 1, :]))
                if p == BASIS:
                    for r in range(NREL):
                        for b, dst in enumerate((w_edge, w_edge2)):
                            cf = coef[:, 2 * r + b:2 * r + b + 1]
                            if r == 0:
                                pre(vec.tensor_scalar(dst[:], et8_i[:], float(r), cf, ALU.is_equal, ALU.mult))
                                pre(vec.tensor_scalar(neg[:], et8_i[:], float(r), cf, ALU.is_equal, ALU.mult))
                            else:
                                pre(vec.tensor_scalar(neg[:], et8_i[:], float(r), cf, ALU.is_equal, ALU.mult))
                                pre(vec.tensor_tensor(dst[:], dst[:], neg[:], ALU.add))
                assert n_pre == PRE[p], (p, n_pre)
                if p:
                    vec.memset(flag[:, 3:4], 0.0).then_inc(consts, 1)
                    dve.wait_ge(consts, 3 + p)
                with dve.Fori(0, ns) as sw:
                    setup_base = dve.snap(sw * SETUP[p])
                    n_set = 0

                    def setup(ins):
                        nonlocal n_set
                        ins.then_inc(s["setup"], 1)
                        n_set += 1
                        if n_set < SETUP[p]:
                            dve.wait_ge(s["setup"], setup_base + n_set)
                    setup(vec.tensor_scalar(base_f[:], base_keep[:], flag[:, 3:4], None, ALU.add))
                    setup(vec.tensor_tensor(rel[:].rearrange("p (q c) -> p q c", c=QUAD),
                                            dst_i[:].rearrange("p (q c) -> p q c", c=QUAD),
                                            base_f[:].unsqueeze(2).broadcast_to([P, NQ, QUAD]), ALU.subtract))
                    if p == GAT:
                        setup(vec.tensor_scalar(neg[:], rel[:], 0.0, None, ALU.is_ge))
                        setup(vec.scalar_tensor_tensor(w_edge[:], rel[:], float(W), neg[:], ALU.is_lt, ALU.mult))
                        setup(vec.tensor_scalar(neg[:], w_edge[:], 1.0, None, ALU.subtract))
                        setup(vec.tensor_scalar(neg[:], neg[:], BIG, None, ALU.mult))
                    setup(vec.tensor_tensor(flag[:, 3:4], flag[:, 3:4], flag[:, 1:2], ALU.add))
                    setup(vec.tensor_copy(base_i[:], base_f[0:1, :]))
                    assert n_set == SETUP[p]
                    with dve.Fori(0, NB) as i:
                        t = dve.snap(sw * NB + i)
                        dve.wait_ge(s["setup"], setup_base + SETUP[p])
                        chain_base = dve.snap(t * CHAIN[p] + PRE[p])
                        n_chain = 0

                        def step(ins):
                            nonlocal n_chain
                            ins.then_inc(chain, 1)
                            n_chain += 1
                            return n_chain

                        def settle():
                            dve.wait_ge(chain, chain_base + n_chain)

                        def firsts(k):
                            return [dve.value_load(base_i[0:1, bass.ds(i * (2 * GQ) + k * GQ + q, 1)], min_val=0,
                                                   max_val=NP - W) for q in range(GQ)]
                        first = {}
                        for k in range(2):
                            cols = bass.ds(i * (2 * G) + k * G, G)
                            hot = wo[k][:, :, 0, :]
                            dve.wait_ge(s["weights_ready", 1 - k], t + k)
                            if p == GAT:
                                first[k] = firsts(k)
                                step(vec.tensor_tensor(oh, iota_w, over_w(rel[:, cols]), ALU.is_equal))
                                step(vec.tensor_tensor(tmp2, iota[:, 0:64].unsqueeze(1).broadcast_to([P, G, 64]),
                                                       over_w(et64_i[:, cols]), ALU.is_equal))
                                settle()
                                for q in range(GQ):
                                    qs = slice(q * QUAD, (q + 1) * QUAD)
                                    step(vec.tensor_tensor(
                                        tmp[:, qs, :], oh[:, qs, :],
                                        H[:, bass.ds(first[k][q], W)].unsqueeze(1).broadcast_to([P, QUAD, W]), ALU.mult))
                                step(vec.tensor_tensor(tmp2, tmp2, c64[:].unsqueeze(1).broadcast_to([P, G, 64]), ALU.mult))
                                settle()
                                step(vec.tensor_reduce(s_q[:], tmp, AX.X, ALU.add))
                                step(vec.tensor_reduce(s_c[:], tmp2, AX.X, ALU.add))
                                settle()
                                step(vec.tensor_tensor(s_q[:], s_q[:], s_c[:], ALU.add))
                                settle()
                                step(vec.tensor_tensor(s_q[:], s_q[:], neg[:, cols], ALU.add))
                                settle()
                                dve.wait_ge(s["landed", k], t * (16 * G) + 16 * G)
                                step(vec.tensor_tensor(att[:, k, :], s_q[:], msgs[k][:, :, D], ALU.add))
                                settle()
                                step(vec.scalar_tensor_tensor(att[:, k, :], att[:, k, :], 0.2, att[:, k, :], ALU.mult, ALU.max))
                                settle()
                                vec.tensor_reduce(gm[:, k:k + 1], att[:, k, :], AX.X, ALU.max).then_inc(gmax_part, 1)
                                dve.wait_ge(gmax_t, t * 2 + (k + 1))
                                vec.tensor_reduce(gx[0:1, k:k + 1], bank[2][0:1, 0:P], AX.X, ALU.max).then_inc(gmax_row, 1)
                                dve.wait_ge(gmax_all, t * 2 + (k + 1))
                                step(vec.tensor_tensor(Rmax[:, k:k + 1], Rmax[:, 1 - k:2 - k], bank[3][:, 0:1], ALU.max))
                                settle()
                                vec.tensor_scalar(nR[:, k:k + 1], Rmax[:, k:k + 1], -1.0, None, ALU.mult).then_inc(shift_ready, 1)
                                vec.tensor_tensor(dR[:, k:k + 1], Rmax[:, 1 - k:2 - k], Rmax[:, k:k + 1], ALU.subtract).then_inc(shift_ready, 1)
                                dve.wait_ge(exp_ready, t * 4 + (2 * k + 2))
                                vec.tensor_tensor(hot, oh, over_w(ex[:, k, :]), ALU.mult).then_inc(s["weights_ready", k], 1)
                            if p == GIN1:
                                step(vec.tensor_tensor(oe[k][:], iota[:, 0:NREL].unsqueeze(1).broadcast_to([P, G, NREL]),
                                                       et8_i[:, cols].unsqueeze(2).broadcast_to([P, G, NREL]), ALU.is_equal))
                                settle()
                                vec.tensor_tensor(hot, iota_w, over_w(rel[:, cols]), ALU.is_equal).then_inc(s["weights_ready", k], 1)
                            if p == GIN2:
                                vec.tensor_tensor(hot, iota_w, over_w(rel[:, cols]), ALU.is_equal).then_inc(s["weights_ready", k], 1)
                                dve.wait_ge(types_loaded, t * 32 + (16 * (k + 1)))
                                vec.tensor_scalar(et_b, et_b.bitcast(I32), pidx[0:NREL, 0:1], None, ALU.is_equal).then_inc(types_hot, 1)
                                dve.wait_ge(picked, t * 2 + (k + 1))
                                dve.wait_ge(s["weights_ready", k], t + 1)
                                for b in range(2):
                                    step(vec.tensor_tensor(tmp[:, 8 * b:8 * b + 8, :], hot[:, 8 * b:8 * b + 8, :],
                                                           bank[4 + b][:].rearrange("p (g w) -> p g w", g=8), ALU.mult))
                                settle()
                                step(vec.tensor_reduce(s_q[:], tmp, AX.X, ALU.add))
                                settle()
                                step(vec.tensor_tensor(w_edge[:, cols], w_edge[:, cols], s_q[:], ALU.add))
                            if p in (RGCN1, RGCN2):
                                step(vec.tensor_tensor(oh, iota_w, over_w(rel[:, cols]), ALU.is_equal))
                                settle()
                                vec.tensor_tensor(hot, oh, over_w(w_edge[:, cols]), ALU.mult).then_inc(s["weights_ready", k], 1)
                            if p == BASIS:
                                step(vec.tensor_tensor(oh, iota_w, over_w(rel[:, cols]), ALU.is_equal))
                                settle()
                                step(vec.tensor_tensor(hot, oh, over_w(w_edge[:, cols]), ALU.mult))
                                settle()
                                vec.tensor_tensor(wo[k][:, :, 1, :], oh, over_w(w_edge2[:, cols]), ALU.mult).then_inc(s["weights_ready", k], 1)
                        for k in range(2):
                            f = first[k] if p == GAT else firsts(k)
                            dve.wait_ge(s["chunk_done", k], t + 1)
                            if p == GAT:
                                dve.wait_ge(rescaled[k], t + 1)
                            for q in range(GQ):
                                o = bank[k][:, q * 2 * W:(q + 1) * 2 * W]
                                win = bass.ds(f[q], W)
                                settle()
                                if q == 0:
                                    dve.wait_ge(s["taken", 1 - k], t + k)
                                if p in (GAT, BASIS):
                                    m = vec.tensor_tensor(acc[:, :, win], acc[:, :, win], o.rearrange("p (a w) -> p a w", a=2), ALU.add)
                                else:
                                    m = vec.tensor_tensor(acc[:, 0, win], acc[:, 0, win], o[:, 0:W], ALU.add)
                                if p == GIN1:
                                    step(m)
                                    m = vec.tensor_tensor(acc[0:NREL, 1, win], acc[0:NREL, 1, win], o[0:NREL, W:2 * W], ALU.add)
                                if q < GQ - 1:
                                    step(m)
                            m.then_inc(s["taken", k], 1)
                        assert n_chain == CHAIN[p], (p, n_chain, CHAIN[p])
                v, a, tt = s["vn"], s["an"], s["tn"]
                KV, KA, KT = (n_steps(p, e) for e in range(3))
                with dve.Fori(0, NT) as i:
                    va, aa, ta = dve.snap(i * KV), dve.snap(i * KA), dve.snap(i * KT)
                    dve.wait_ge(s["taken", 1], ns * NB)

                    def after(sm, base, e, name, h):
                        dve.wait_ge(sm, base + step_at(p, e, name, h))

                    def col(h):
                        return bass.ds(i * TURN + HOFF[h], HALF[h])
                    if p == GAT:
                        for h in range(2):
                            dve.wait_ge(tt, ta)
                            dve.wait_ge(a, aa)
                            vec.tensor_scalar(part(1, h), acc[:, 1, col(h)], 1e-10, None, ALU.add).then_inc(v, 1)
                        for h in range(2):
                            after(v, va, 0, "guard", h)
                            vec.reciprocal(part(4, h), part(1, h)).then_inc(v, 1)
                        for h in range(2):
                            after(v, va, 0, "recip", h)
                            vec.tensor_tensor(part(0, h), acc[:, 0, col(h)], part(4, h), ALU.mult).then_inc(v, 1)
                        for h in range(2):
                            after(tt, ta, 2, "lin", h)
                            vec.tensor_tensor(part(2, h), bank[2 + h][:, 0:HALF[h]], X[:, col(h)], ALU.add).then_inc(v, 1)
                    if p in (GIN1, GIN2):
                        for h in range(2):
                            dve.wait_ge(tt, ta)
                            dve.wait_ge(a, aa)
                            vec.tensor_tensor(part(0, h), acc[:, 0, col(h)], (X if p == GIN1 else H)[:, col(h)], ALU.add).then_inc(v, 1)
                    if p == GIN1:
                        for h in range(2):
                            after(a, aa, 1, "outr", h)
                            vec.tensor_copy(H[:, col(h)], part(5, h)).then_inc(v, 1)
                    if p == GIN2:
                        for h in range(2):
                            after(tt, ta, 2, "lin2", h)
                            vec.scalar_tensor_tensor(part(2, h), bank[4 + h][:, 0:HALF[h]], bcol("b2b"), X[:, col(h)],
                                                     ALU.add, ALU.add).then_inc(v, 1)
                    if p == RGCN1:
                        for h in range(2):
                            after(tt, ta, 2, "lin", h)
                            dve.wait_ge(a, aa)
                            vec.tensor_tensor(part(2, h), bank[2 + h][:, 0:HALF[h]], acc[:, 0, col(h)], ALU.add).then_inc(v, 1)
                        for h in range(2):
                            after(a, aa, 1, "outr", h)
                            vec.tensor_copy(H[:, col(h)], part(5, h)).then_inc(v, 1)
                    if p == RGCN2:
                        for h in range(2):
                            after(tt, ta, 2, "lin", h)
                            vec.tensor_tensor(part(0, h), bank[2 + h][:, 0:HALF[h]], acc[:, 0, col(h)], ALU.add).then_inc(v, 1)
                        for h in range(2):
                            after(v, va, 0, "sum0", h)
                            vec.scalar_tensor_tensor(part(2, h), part(0, h), bcol("bias1"), X[:, col(h)], ALU.add, ALU.add).then_inc(v, 1)
                    if p == BASIS:
                        for h in range(2):
                            after(tt, ta, 2, "lin", h)
                            vec.scalar_tensor_tensor(part(2, h), bank[2 + h][:, 0:HALF[h]], bcol("h_bias"), X[:, col(h)],
                                                     ALU.add, ALU.add).then_inc(v, 1)
                    if p in NORMED:
                        mb = 2 if p == GIN2 else 4
                        for h in range(2):
                            after(tt, ta, 2, "mean", h)
                            after(v, va, 0, "sum", h)
                            vec.tensor_tensor(part(3, h), part(2, h), bank[mb + h][:, 0:HALF[h]], ALU.subtract).then_inc(v, 1)
                        for h in range(2):
                            after(a, aa, 1, "std", h)
                            vec.reciprocal(part(0, h), part(1, h)).then_inc(v, 1)
                        for h in range(2):
                            after(v, va, 0, "rstd", h)
                            if p in ROWS:
                                dve.wait_ge(s["rows_ready", h], i)
                            if p in WIDE:
                                dve.wait_ge(s["hi_ready"], i * 7)
                            if p == BASIS:
                                dve.wait_ge(out_stored[h], i * 16)
                            vec.tensor_tensor(part(5, h), part(3, h), part(0, h), ALU.mult).then_inc(v, 1)
                    if p in WIDE:
                        for k in range(7):
                            dve.wait_ge(s["hi_ready"], i * 7 + (k + 1))
                            dve.wait_ge(s["wide_stored", k % 4], i * (16 * len(range(k % 4, 7, 4))) + 16 * (k // 4))
                            vec.tensor_copy(wide_rows[k % 4][:, 512:1024], bank[1][:]).then_inc(s["hi_taken"], 1)


INS = ["x_rows", "xT", "src_pt", "dst_pt", "dst_q", "et64_pt", "et8_pt", "et8_flat", "mats", "bias", "avec", "relT",
       "tw0", "tw1", "coeff"]


def lay_out(x, src, dst, edge_type_64, edge_type_8, w):
    N, E = x.shape[0], src.shape[0]
    NP, NCH = sizes(N, E)

    def padded(a, fill):
        return np.concatenate([a, np.full(NCH * P - E, fill, a.dtype)])

    def pt(a):
        return np.ascontiguousarray(a.reshape(NCH, P).T)
    d, e8 = padded(dst, 4 * NP), padded(edge_type_8, 0)
    return {
        "x_rows": np.concatenate([x, np.zeros((NP - N, D), x.dtype)]),
        "xT": np.ascontiguousarray(np.concatenate([x, np.zeros((NP - N, D), x.dtype)]).T),
        "src_pt": pt(padded(src, 0)), "dst_pt": pt(d), "dst_q": d.reshape(NCH // QUAD // 2, 2 * QUAD * P),
        "et64_pt": pt(padded(edge_type_64, 0)), "et8_pt": pt(e8), "et8_flat": e8.reshape(1, -1),
        "mats": np.concatenate([w["L0_gnn_W"], w["L1_gnn_W1a"], w["L1_gnn_W1b"], w["L1_gnn_W2a"], w["L1_gnn_W2b"],
                                w["L2_gnn_roots"][0], w["L2_gnn_roots"][1], w["L3_gnn_W"][0], w["L3_gnn_W"][1],
                                w["L3_gnn_W"][2], w["L3_gnn_loop_weight"], w["L0_gnn_W"].T, w["L0_gnn_W_r"].T], axis=1),
        "bias": np.stack([w["L1_gnn_b1a"], w["L1_gnn_b1b"], w["L1_gnn_b2a"], w["L1_gnn_b2b"], w["L2_gnn_biases"][0],
                          w["L2_gnn_biases"][1], w["L3_gnn_h_bias"]], axis=1),
        "avec": np.ascontiguousarray(w["L0_gnn_a"].reshape(3, D).T),
        "relT": np.ascontiguousarray(w["L0_gnn_rel_emb"].T),
        "tw0": np.concatenate(list(w["L2_gnn_weights"][0]), axis=1),
        "tw1": np.concatenate(list(w["L2_gnn_weights"][1]), axis=1),
        "coeff": np.ascontiguousarray(w["L3_gnn_coeff"].reshape(1, -1)),
    }


def kernel(x, src, dst, edge_type_64, edge_type_8, **weights):
    import concourse.bacc as bacc
    from concourse.bass_utils import run_bass_kernel_spmd

    x, src, dst, e64, e8 = (np.asarray(a) for a in (x, src, dst, edge_type_64, edge_type_8))
    N, E = x.shape[0], src.shape[0]
    arrays = lay_out(x, src, dst, e64, e8, {k: np.asarray(v) for k, v in weights.items()})
    nc = bacc.Bacc("TRN2", target_bir_lowering=False, num_devices=1)
    args = [nc.dram_tensor(n, arrays[n].shape, mybir.dt.from_np(arrays[n].dtype), kind="ExternalInput").ap() for n in INS]
    outT = nc.dram_tensor("outT", [P, sizes(N, E)[0]], F32, kind="ExternalOutput").ap()
    with nc.allow_non_contiguous_dma("columns of small arrays"):
        build(nc, N, E, *args, outT)
    r = run_bass_kernel_spmd(nc, [arrays], core_ids=[0])
    return np.ascontiguousarray(r.results[0]["outT"][:, :N].T)
```

```python
import numpy as np
import concourse.bass as bass
from concourse import mybir

F32 = mybir.dt.float32
I32 = mybir.dt.int32
ALU = mybir.AluOpType
ACT = mybir.ActivationFunctionType
AX = mybir.AxisListType

P = 128
D = 128
W = 64
QUAD = 4
G = 16
GQ = G // QUAD
TURN = 4 * P
NREL = 8
BIG = 1.0e30
LOWEST = -3.0e38


def round_up(a, b):
    return (a + b - 1) // b * b


def sizes(n_nodes, n_edges):
    return round_up(n_nodes, P), round_up(-(-n_edges // P), 2 * G)


MATS = ["W", "W1a", "W1b", "W2a", "W2b", "root0", "root1", "V0", "V1", "V2", "loop", "WT", "WrT"]
BIAS = ["b1a", "b1b", "b2a", "b2b", "bias0", "bias1", "h_bias"]

GAT, GIN1, GIN2, RGCN1, RGCN2, BASIS = range(6)
FRONT = {
    GAT: (["guard", "recip", "norm", "sum"], [], ["lin"]),
    GIN1: (["zin", "keep"], ["hidden", "outr"], ["lin", "lin2"]),
    GIN2: (["zin", "sum"], ["hidden"], ["lin", "lin2"]),
    RGCN1: (["sum", "keep"], ["outr"], ["lin"]),
    RGCN2: (["sum0", "sum"], [], ["lin"]),
    BASIS: (["sum"], [], ["lin"]),
}
NORMED = (GAT, GIN2, RGCN2, BASIS)
ROWS = (GAT, GIN1, RGCN2)
WIDE = (GIN2, RGCN1)


def steps_of(p):
    v, a, t = (list(x) for x in FRONT[p])
    if p in NORMED:
        v += ["center", "rstd", "out"]
        a += ["square", "std", "store"]
        t += ["mean", "var"]
    if p != BASIS:
        v += ["zero"]
    return v, a, t


def build(nc, N, E, x_rows, xT, src_pt, dst_pt, dst_q, et64_pt, et8_pt, et8_flat, mats, bias, avec, relT, tw0, tw1,
          coeff, outT):
    NP, NCH = sizes(N, E)
    NQ = NCH // QUAD
    QP = NQ // 2
    NB = NCH // (2 * G)
    FULL = (NP - 3 * P - 1) // TURN
    rest = NP - FULL * TURN
    last = 3 * P if rest >= 5 * P else 2 * P
    NT = FULL + 2
    TAIL_TILES = [(FULL, FULL * TURN, rest - last), (FULL + 1, NP - last, last)]
    NSW = NP // W
    C = min(max(1, TURN * E // (N * 2 * G * P)), (NB - 1) // FULL)
    LAG = max(0, min(-(-FULL * TURN * E // (N * 2 * G * P)), NB - 1) - FULL * C)
    QT = 2 * GQ
    from contextlib import ExitStack
    ctx = ExitStack()
    with ctx:
        def sb(name, shape, dt=F32):
            return ctx.enter_context(nc.sbuf_tensor(name, shape, dt))

        def sem(name):
            return ctx.enter_context(nc.semaphore(name))

        def dram(name, shape, dt=F32):
            return nc.dram_tensor(name, shape, dt, kind="Internal").ap()

        table0 = dram("table0", [NP, D + 1])
        table_gin1 = dram("table_gin1", [NP, D])
        table_gin2 = dram("table_gin2", [NP, D])
        table_rel1 = dram("table_rel1", [NP * NREL, D])
        table_rel2 = dram("table_rel2", [NP * NREL, D])
        table_basis = dram("table_basis", [NP, D])
        base_d = dram("base_d", [1, NQ])
        wide_d = dram("wide_d", [1, QP])
        tables = {GAT: table0, GIN1: table_gin1, GIN2: table_gin2, RGCN1: table_rel1, RGCN2: table_rel2,
                  BASIS: table_basis}
        next_table = {GAT: table_gin1, GIN1: table_gin2, GIN2: table_rel1, RGCN1: table_rel2, RGCN2: table_basis}

        acc = sb("acc", [P, 2, NP])
        X = sb("X", [P, NP])
        H = sb("H", [P, NP])
        msgs = [sb(f"msgs{k}", [P, G, D + 1]) for k in range(2)]
        wo = [sb(f"wo{k}", [P, 2, G, W]) for k in range(2)]
        idx = [sb(f"idx{k}", [P, G], I32) for k in range(2)]
        work = sb("work", [P, max(6 * TURN, 3 * G * W + G * P)])
        src_i = sb("src_i", [P, NCH], I32)
        dst_i = sb("dst_i", [P, NCH], I32)
        et64_i = sb("et64_i", [P, NCH], I32)
        row_i = et64_i
        et8_i = sb("et8_i", [P, NCH], I32)
        rel = sb("rel", [P, NCH])
        w_edge = sb("w_edge", [P, NCH])
        w_edge2 = sb("w_edge2", [P, NCH])
        neg = w_edge2
        base_keep = sb("base_keep", [P, NQ])
        base_f = sb("base_f", [P, NQ])
        base_i = sb("base_i", [1, NQ], I32)
        wide = sb("wide", [P, QP])
        chk = sb("chk", [P, NT])
        flag = sb("flag", [P, 4])
        flag_i = sb("flag_i", [1, 1], I32)
        bq = sb("bq", [QP, 2])
        mq = sb("mq", [QP, 2])
        wq = sb("wq", [QP, 1])
        m_sb = sb("m_sb", [P, len(MATS), D])
        b_sb = sb("b_sb", [P, len(BIAS)])
        a_sb = sb("a_sb", [P, 3])
        relT_sb = sb("relT_sb", [P, 64])
        tw = sb("tw", [P, NREL * D])
        coef = sb("coef", [P, NREL * 2])
        vv = sb("vv", [P, 3])
        v3b = sb("v3b", [P, P])
        u2b = sb("u2b", [P, P])
        c64 = sb("c64", [P, 64])
        pcol = sb("pcol", [P, NP // P])
        iota_i = sb("iota_i", [P, P], I32)
        iota = sb("iota", [P, P])
        pidx_i = sb("pidx_i", [P, 1], I32)
        pidx = sb("pidx", [P, 1])
        ident = sb("ident", [P, P])
        ones = sb("ones", [P, P])
        mean_m = sb("mean_m", [P, P])
        oe = [sb(f"oe{k}", [P, G, NREL]) for k in range(2)]
        s_q = sb("s_q", [P, G])
        s_c = sb("s_c", [P, G])
        att = sb("att", [P, 2, G])
        ex = sb("ex", [P, 2, G])
        gm = sb("gm", [P, 2])
        gx = sb("gx", [1, 2])
        Rmax = sb("Rmax", [P, 2])
        dR = sb("dR", [P, 2])
        nR = sb("nR", [P, 2])
        alpha = sb("alpha", [P, 2])
        stage = [sb(f"stage{k}", [P, NREL * D])[:, :] for k in range(2)]
        stage += [wo[k][:, 1, :, :].rearrange("p g w -> p (g w)") for k in range(2)]
        eps = sb("eps", [P, 1])

        oh = work[:, 0:G * W].rearrange("p (g w) -> p g w", g=G)
        tmp = work[:, G * W:2 * G * W].rearrange("p (g w) -> p g w", g=G)
        LG = W + 64 + 2
        logit = work[:, G * W:G * W + G * LG].rearrange("p (g w) -> p g w", g=G)
        assert 6 * TURN <= 3 * G * W
        part_edges = work[:, 0:NCH]
        et_b = work[0:NREL, 3 * G * W:3 * G * W + G * P]

        def tile(i, first=None, n=TURN):
            half = -(-n // (2 * P)) * P
            rows0 = i * (TURN // P) if first is None else first // P
            return [(0, 0, half), (1, half, n - half)], i * TURN if first is None else first, rows0, n // P

        def slot(i, k, first=None, n=TURN):
            if first is None:
                return k, i * 16
            return (first // P + k) % 4, 16 * ((first // P + k) // 4)

        def part(k, h, n):
            return work[:, k * TURN + h * (TURN // 2):k * TURN + h * (TURN // 2) + n]
        bank = [ctx.enter_context(nc.psum_tensor(f"bank{k}", [P, 512], F32)) for k in range(8)]

        def mat(name):
            return m_sb[:, MATS.index(name), :]

        def bcol(name):
            k = BIAS.index(name)
            return b_sb[:, k:k + 1]

        loaded = sem("loaded")
        idx_ready = [sem(f"idx_ready{k}") for k in range(2)]
        landed = [sem(f"landed{k}") for k in range(2)]
        prep = sem("prep")
        gathering = sem("gathering")
        tile_read = sem("tile_read")
        waited = sem("waited")
        emptied = sem("emptied")
        used_up = sem("used_up")
        x_copied = sem("x_copied")
        pcol_out = sem("pcol_out")
        consts = sem("consts")
        v0 = sem("v0")
        a0 = sem("a0")
        t0 = sem("t0")
        based = sem("based")
        based_back = sem("based_back")
        S = [dict() for _ in range(6)]
        for p in range(6):
            for k in range(2):
                for n in ( "weights_ready", "chunk_done", "taken"):
                    S[p][n, k] = sem(f"{n}{k}_{p}")
                if p in ROWS:
                    for n in ("rows_ready", "rows_copied", "rows_stored"):
                        S[p][n, k] = sem(f"{n}{k}_{p}")
            for n in ("setup", "chain", "sums", "vn", "an", "tn"):
                S[p][n] = sem(f"{n}_{p}")
            if p in WIDE:
                for n in ("lo_ready", "hi_ready", "lo_taken", "hi_taken"):
                    S[p][n] = sem(f"{n}_{p}")
                for k in range(4):
                    S[p]["wide_stored", k] = sem(f"wide_stored{k}_{p}")
        gmax_part, gmax_t, gmax_row, gmax_all, shift_ready, exp_ready = (
            sem(n) for n in ("gmax_part", "gmax_t", "gmax_row", "gmax_all", "shift_ready", "exp_ready"))
        rescaled = [sem(f"rescaled{k}") for k in range(2)]
        types_loaded, types_hot, picked, pick_taken = (
            sem(n) for n in ("types_loaded", "types_hot", "picked", "pick_taken"))
        rows_made = sem("rows_made")
        acc_zeroed = sem("acc_zeroed")
        tw_loaded = sem("tw_loaded")
        out_stored = [sem(f"out_stored{h}") for h in range(2)]

        NLOAD = 13
        block = ctx.enter_context(nc.Block())

        def sweeping(eng):
            eng.wait_ge(v0, V0["flag_i"])
            f = eng.value_load(flag_i[0:1, 0:1], min_val=0, max_val=1)
            return f, eng.snap(f * (NSW * NB))

        def windows(eng, group):
            _, first = nc.values_load_multi_w_load_instructions(
                base_i[0:1, bass.ds(group * GQ, GQ)], engines=(eng.engine,), min_val=0, max_val=NP - W,
                skip_runtime_bounds_check_because="VectorE clamps them to 0 .. NP - W")
            return first

        def edge_pass(eng, p, needed, off, turn, node, setup=None, restore=None, flush=None,
                      main=None, begin=None, end=None):
            def run(lo, hi, before):
                if begin:
                    begin(before)
                if flush is None:
                    with eng.Fori(lo, hi) as T:
                        turn(T, eng.snap(before + T), False)
                    if end and hi == NB:
                        end(hi - 1, eng.snap(before + (hi - 1)))
                    return
                turn(lo, eng.snap(before + lo), True)
                if hi > lo + 1:
                    with eng.Fori(lo + 1, hi) as T:
                        turn(T, eng.snap(before + T), False)
                flush(hi - 1, eng.snap(before + (hi - 1)))
            with eng.If(needed > 0):
                with eng.Fori(0, NSW) as sw:
                    if setup:
                        setup(sw)
                    run(0, NB, eng.snap(sw * NB))
                if restore:
                    restore()
            if main:
                main()
            if p == GAT:
                run(0, NB, off)
                if node:
                    with eng.Fori(0, FULL) as j:
                        node(j, eng.snap(off + NB))
                    for n_tile in TAIL_TILES:
                        node(n_tile[0], eng.snap(off + NB), *n_tile[1:])
                return
            if begin:
                begin(off)
            if LAG:
                with eng.Fori(0, LAG) as T:
                    turn(T, eng.snap(off + T), False)
            with eng.Fori(0, FULL) as j:
                first = eng.snap(j * C + LAG)
                with eng.Fori(0, C) as u:
                    T = eng.snap(first + u)
                    turn(T, eng.snap(off + T), False)
                if node:
                    node(j, eng.snap(off + first + C))
            with eng.Fori(FULL * C + LAG, NB - 1) as T:
                turn(T, eng.snap(off + T), False)
            if node:
                node(TAIL_TILES[0][0], eng.snap(off + (NB - 1)), *TAIL_TILES[0][1:])
            run(NB - 1, NB, off)
            if node:
                node(TAIL_TILES[1][0], eng.snap(off + NB), *TAIL_TILES[1][1:])

        def n_steps(p, e):
            return 2 * len(steps_of(p)[e])

        def step_at(p, e, name, h):
            return 2 * steps_of(p)[e].index(name) + h + 1

        V0 = {n: k + 1 for k, n in enumerate(
            ["iota", "pidx", "ident", "ones", "mean", "qmin", "qcl", "qmsk", "qmax", "qspan", "qwide", "vv", "v3b", "u2b",
             "c64", "pcol", "spans", "wide"] + [f"late{j}{x}" for j in range(NT - 1) for x in "ab"] +
            ["flag", "far", "keepf", "base_keep", "flag_i", "base_i", "base_f", "rel", "neg1", "neg2", "neg3", "neg4",
             "off", "R", "eps"])}
        T0 = {n: k + 1 for k, n in enumerate(["vv", "c64", "pcol"])}
        TQ = len(T0)
        SETUP = {p: (8 if p == GAT else 4) for p in range(6)}
        CHAIN = {GAT: 2 * 12, GIN1: 2, GIN2: 2 * 3, RGCN1: 2, RGCN2: 2, BASIS: 2 * 2}
        SUMS = {p: GQ - 1 + (GQ if p == GIN1 else 0) for p in range(6)}
        TAILS = TURN // P
        TAILS_IN_ALL = NP // P

        @block.sync
        def _(sp):
            for dst, src in ((X[:], xT), (src_i[:], src_pt), (dst_i[:], dst_pt), (et64_i[:], et64_pt),
                             (et8_i[:], et8_pt), (m_sb[:], mats.rearrange("p (k d) -> p k d", d=D)), (b_sb[:], bias),
                             (a_sb[:], avec), (relT_sb[:], relT), (tw[:], tw0),
                             (coef[:], coeff.to_broadcast([P, NREL * 2])),
                             (work[0:QP, 0:2 * QUAD * P].bitcast(I32), dst_q)):
                sp.dma_start(dst, src).then_inc(loaded, 16)
            sp.dma_start(work[0:1, 4 * QUAD * P:4 * QUAD * P + 16], mats[0:1, 0:16]).then_inc(loaded, 16)
            sp.wait_ge(v0, V0["qwide"])
            sp.dma_start(base_d.rearrange("o (p k) -> (o p) k", k=2), bq[:]).then_inc(based, 16)
            sp.dma_start(wide_d.rearrange("o p -> p o"), wq[:]).then_inc(based, 16)
            sp.wait_ge(based, 32)
            sp.dma_start(base_keep[:], base_d.to_broadcast([P, NQ])).then_inc(based_back, 16)
            sp.dma_start(wide[:], wide_d.to_broadcast([P, QP])).then_inc(based_back, 16)
            sp.wait_ge(v0, V0["pcol"])
            sp.dma_start(table0.rearrange("(t p) c -> p t c", p=P)[:, :, D:D + 1],
                         pcol[:].unsqueeze(2)).then_inc(pcol_out, 16)
            needed, off = sweeping(sp)
            for p in range(6):
                s = S[p]
                rows = row_i if p in (RGCN1, RGCN2) else src_i
                if p == RGCN1:
                    sp.wait_ge(rows_made, 1)
                    sp.wait_ge(S[GIN2]["hi_ready"], TAILS_IN_ALL)
                    sp.dma_start(tw[:], tw1).then_inc(tw_loaded, 16)

                if p:
                    for k in range(2):
                        sp.wait_ge(S[p - 1]["chunk_done", k], off + NB)
                    sp.sem_inc(tile_read, 1)

                def turn(T, t, _):
                    for k in range(2):
                        sp.wait_ge(s["chunk_done", k], t)
                        sp.dma_start(idx[k][:], rows[:, bass.ds(T * (2 * G) + k * G, G)]).then_inc(idx_ready[k], 16)
                        if p == GIN2:
                            sp.wait_ge(picked, t * 2 + k)
                            sp.dma_start(et_b.bitcast(I32),
                                         et8_flat[0:1, bass.ds(T * (2 * G * P) + k * G * P, G * P)].to_broadcast(
                                             [NREL, G * P])).then_inc(types_loaded, 16)

                edge_pass(sp, p, needed, off, turn, None)
            for h in range(2):
                sp.wait_ge(out_stored[h], 16 * NT)

        @block.gpsimd
        def _(pool):
            pool.dma_start(table0[:, 0:D], x_rows).then_inc(x_copied, 16)
            pool.iota(iota_i[:], pattern=[[1, P]], base=0, channel_multiplier=0).then_inc(consts, 1)
            pool.iota(pidx_i[:], pattern=[[0, 1]], base=0, channel_multiplier=1).then_inc(consts, 1)
            pool.wait_ge(x_copied, 16)
            pool.wait_ge(pcol_out, 16)
            needed, off = sweeping(pool)
            for p in range(6):
                s = S[p]
                if p and p - 1 in ROWS:
                    for h in range(2):
                        pool.wait_ge(S[p - 1]["rows_stored", h], 16 * NT)
                if p and p - 1 in WIDE:
                    for k in range(4):
                        pool.wait_ge(S[p - 1]["wide_stored", k], 16 * len(range(k, TAILS_IN_ALL, 4)))
                width = D + 1 if p == GAT else D

                def turn(T, t, _):
                    for k in range(2):
                        pool.wait_ge(idx_ready[k], (off + NB) * (16 * p) + t * 16 + 16)
                        pool.wait_ge(s["chunk_done", k], t)
                        pool.wait_ge(emptied, (off + NB) * p + swept[0])
                        pool.sem_inc(gathering, 1)
                        for c in range(G):
                            pool.indirect_dma_start(
                                out=msgs[k][:, c, 0:width], out_offset=None, in_=tables[p],
                                in_offset=bass.IndirectOffsetOnAxis(ap=idx[k][:, c:c + 1], axis=0)).then_inc(
                                    landed[k], 16)
                def settled(_, t):
                    for k in range(2):
                        pool.wait_ge(s["chunk_done", k], t + 1)
                    pool.sem_inc(used_up, 1)
                    pool.inc_swdge_sem(landed, [16 * G * NB] * 2, mode="sub").then_inc(emptied, NB)
                swept = [0]

                def begin(before):
                    swept[0] = before
                edge_pass(pool, p, needed, off, turn, None, begin=begin, end=settled)

        @block.scalar
        def _(act):
            def q_out(i, *place):
                hs, first, _, _ = tile(i, *place)
                for h, o, n in hs:
                    act.wait_ge(t0, i * 2 + (TQ + h + 1))
                    nc.scalar.activation(H[:, bass.ds(first + o, n)], bank[2 + h][:, 0:n], ACT.Copy).then_inc(a0, 1)
            with act.Fori(0, FULL) as i:
                q_out(i)
            for n_tile in TAIL_TILES:
                q_out(*n_tile)
            needed, off = sweeping(act)
            for p in range(6):
                s = S[p]
                v, a, tt = s["vn"], s["an"], s["tn"]
                KV, KA, KT = (n_steps(p, e) for e in range(3))

                def turn(T, t, _):
                    for k in range(2):
                        act.wait_ge(shift_ready, t * 4 + (2 * k + 2))
                        nc.scalar.activation(alpha[:, k:k + 1], dR[:, k:k + 1], ACT.Exp).then_inc(exp_ready, 1)
                        nc.scalar.activation(ex[:, k, :], att[:, k, :], ACT.Exp, bias=nR[:, k:k + 1]).then_inc(exp_ready, 1)
                        act.wait_ge(exp_ready, t * 4 + (2 * k + 1))
                        act.wait_ge(s["taken", 1 - k], t + k)
                        flat = acc[:].rearrange("p a n -> p (a n)")
                        nc.scalar.activation(flat, flat, ACT.Copy, scale=alpha[:, k:k + 1]).then_inc(rescaled[k], 1)

                def node(i, t, *place):
                    hs, first, rows0, tails = tile(i, *place)
                    va, aa, ta = act.snap(i * KV), act.snap(i * KA), act.snap(i * KT)

                    def after(sm, base, e, name, h):
                        act.wait_ge(sm, base + step_at(p, e, name, h))

                    def col(h):
                        return bass.ds(first + hs[h][1], hs[h][2])
                    if p in (GIN1, GIN2):
                        for h, o, n in hs:
                            after(tt, ta, 2, "lin", h)
                            nc.scalar.activation(part(1, h, n), bank[2 + h][:, 0:n], ACT.Relu,
                                                 bias=bcol("b1a" if p == GIN1 else "b2a")).then_inc(a, 1)
                    if p == GIN1:
                        for h, o, n in hs:
                            after(tt, ta, 2, "lin2", h)
                            act.wait_ge(v, va)
                            act.wait_ge(s["rows_ready", h], i)
                            nc.scalar.activation(part(5, h, n), bank[4 + h][:, 0:n], ACT.Relu, bias=bcol("b1b")).then_inc(a, 1)
                    if p == RGCN1:
                        for h, o, n in hs:
                            after(v, va, 0, "sum", h)
                            act.wait_ge(s["hi_ready"], rows0)
                            nc.scalar.activation(part(5, h, n), part(2, h, n), ACT.Relu, bias=bcol("bias0")).then_inc(a, 1)
                    if p in NORMED:
                        for h, o, n in hs:
                            after(v, va, 0, "center", h)
                            nc.scalar.activation(part(4, h, n), part(3, h, n), ACT.Square).then_inc(a, 1)
                        for h, o, n in hs:
                            after(tt, ta, 2, "var", h)
                            nc.scalar.activation(part(1, h, n), bank[6 + h][:, 0:n], ACT.Sqrt, bias=eps[:, 0:1]).then_inc(a, 1)
                        for h, o, n in hs:
                            after(v, va, 0, "out", h)
                            nc.scalar.activation(X[:, col(h)], part(5, h, n), ACT.Copy).then_inc(a, 1)
                    if p == BASIS:
                        for h, o, n in hs:
                            after(v, va, 0, "out", h)
                            act.dma_start(outT[:, col(h)], part(5, h, n)).then_inc(out_stored[h], 16)
                    if p in ROWS:
                        view = next_table[p].rearrange("(t p) c -> p t c", p=P)
                        for h, o, n in hs:
                            rows = stage[h][:, 0:n]
                            act.wait_ge(s["rows_ready", h], i + 1)
                            act.wait_ge(s["rows_stored", h], i * 16)
                            nc.scalar.activation(rows, bank[h][:, 0:n], ACT.Copy).then_inc(s["rows_copied", h], 1)
                            act.wait_ge(s["rows_copied", h], i + 1)
                            act.dma_start(view[:, bass.ds(rows0 + o // P, n // P), :],
                                          rows.rearrange("p (t c) -> p t c", c=D)).then_inc(s["rows_stored", h], 16)
                    if p in WIDE:
                        view = next_table[p].rearrange("(t p r) c -> p t (r c)", p=P, r=NREL)

                        def store(k):
                            act.wait_ge(s["lo_taken"], rows0 + (k + 1))
                            act.wait_ge(s["hi_taken"], rows0 + (k + 1))
                            b, _ = slot(i, k, *place)
                            act.dma_start(view[:, bass.ds(rows0 + k, 1), :],
                                          stage[b].unsqueeze(1)).then_inc(s["wide_stored", b], 16)
                        for k in range(tails):
                            act.wait_ge(s["lo_ready"], rows0 + (k + 1))
                            b, stored = slot(i, k, *place)
                            act.wait_ge(s["wide_stored", b], stored)
                            nc.scalar.activation(stage[b][:, 0:512], bank[0][:], ACT.Copy).then_inc(s["lo_taken"], 1)
                            if k:
                                store(k - 1)
                        store(tails - 1)
                if p == GAT:
                    act.wait_ge(acc_zeroed, 1)
                    edge_pass(act, p, needed, off, turn, node)
                else:
                    with act.Fori(0, FULL) as j:
                        node(j, None)
                    for n_tile in TAIL_TILES:
                        node(n_tile[0], None, *n_tile[1:])

        @block.tensor
        def _(pe):
            pe.wait_ge(loaded, 16 * NLOAD)
            pe.matmul(bank[0][:, 0:1], mat("WT"), a_sb[:, 0:1], start=True, stop=True)
            pe.matmul(bank[0][:, 1:2], mat("WrT"), a_sb[:, 1:2], start=True, stop=True)
            pe.matmul(bank[0][:, 2:3], mat("WT"), a_sb[:, 2:3], start=True, stop=True).then_inc(t0, 1)
            pe.wait_ge(v0, V0["u2b"])
            pe.matmul(bank[1][:, 0:64], u2b[:], relT_sb[:], start=True, stop=True).then_inc(t0, 1)
            for n in range(NP // P):
                m = pe.matmul(bank[4][:, n:n + 1], X[:, n * P:(n + 1) * P], vv[:, 0:1], start=True, stop=True)
            m.then_inc(t0, 1)

            def q_in(i, *place):
                hs, first, _, _ = tile(i, *place)
                for h, o, n in hs:
                    pe.wait_ge(a0, i * 2)
                    pe.matmul(bank[2 + h][:, 0:n], v3b[:], X[:, bass.ds(first + o, n)],
                              start=True, stop=True).then_inc(t0, 1)
            with pe.Fori(0, FULL) as i:
                q_in(i)
            for n_tile in TAIL_TILES:
                q_in(*n_tile)
            needed, off = sweeping(pe)
            pe.wait_ge(a0, 2 * NT)
            for p in range(6):
                s = S[p]
                v, a, tt = s["vn"], s["an"], s["tn"]
                KV, KA, KT = (n_steps(p, e) for e in range(3))

                placed = [None]

                def turn(T, t, _):
                    for k in range(2):
                        if p == GAT:
                            pe.wait_ge(gmax_part, t * 2 + (k + 1))
                            pe.matmul(bank[2][0:1, 0:P], gm[:, k:k + 1], ident[:], start=True, stop=True).then_inc(gmax_t, 1)
                            pe.wait_ge(gmax_row, t * 2 + (k + 1))
                            pe.matmul(bank[3][:, 0:1], ones[0:1, :], gx[0:1, k:k + 1], start=True, stop=True).then_inc(gmax_all, 1)
                        pe.wait_ge(s["weights_ready", k], t + 1)
                        pe.wait_ge(gathering, (off + NB) * (2 * p) + t * 2 + (k + 1))
                        pe.sem_inc(waited, 1)
                        pe.wait_ge(landed[k], T * (16 * G) + 16 * G)
                        pe.wait_ge(s["taken", k], t)
                        for q in range(GQ):
                            o = bank[k][:, q * 2 * W:(q + 1) * 2 * W]
                            for c in range(q * QUAD, (q + 1) * QUAD):
                                st = dict(start=c % QUAD == 0, stop=c % QUAD == QUAD - 1)
                                if p == BASIS:
                                    m = pe.matmul(o.rearrange("p (a w) -> p a w", a=2), msgs[k][:, c, 0:D], wo[k][:, :, c, :], **st)
                                else:
                                    m = pe.matmul(o[:, 0:W], msgs[k][:, c, 0:D], wo[k][:, 0, c, :], **st)
                            for c in range(q * QUAD, (q + 1) * QUAD):
                                st = dict(start=c % QUAD == 0, stop=c % QUAD == QUAD - 1)
                                if p == GAT:
                                    m = pe.matmul(o[:, W:2 * W], ones[:], wo[k][:, 0, c, :], **st)
                                if p == GIN1:
                                    m = pe.matmul(o[0:NREL, W:2 * W], oe[k][:, c, :], wo[k][:, 0, c, :], **st)
                        m.then_inc(s["chunk_done", k], 1)
                        if p == GIN2:
                            pe.wait_ge(s["setup"], placed[0])
                            pe.sem_inc(waited, 1)
                            first = windows(pe, T * 2 + k)
                            pe.wait_ge(types_hot, t * 2 + (k + 1))
                            pe.wait_ge(pick_taken, t * 2 + k)
                            for c in range(G):
                                m = pe.matmul(bank[4 + c // 8][:, (c % 8) * W:(c % 8 + 1) * W],
                                              et_b[:, c * P:(c + 1) * P], acc[0:NREL, 1, bass.ds(first[c // QUAD], W)],
                                              start=True, stop=True)
                            m.then_inc(picked, 1)

                def node(i, t, *place):
                    hs, first, rows0, tails = tile(i, *place)
                    va, aa, ta = pe.snap(i * KV), pe.snap(i * KA), pe.snap(i * KT)
                    for k in range(2):
                        pe.wait_ge(s["taken", k], t)

                    def after(sm, base, e, name, h):
                        pe.wait_ge(sm, base + step_at(p, e, name, h))

                    def col(h):
                        return bass.ds(first + hs[h][1], hs[h][2])
                    pe.wait_ge(v, va)
                    pe.wait_ge(a, aa)
                    for h, o, n in hs:
                        out = bank[2 + h][:, 0:n]
                        if p == GAT:
                            after(v, va, 0, "norm", h)
                            pe.matmul(out, mat("W"), part(0, h, n), start=True, stop=True).then_inc(tt, 1)
                        if p in (GIN1, GIN2):
                            after(v, va, 0, "zin", h)
                            pe.matmul(out, mat("W1a" if p == GIN1 else "W2a"), part(0, h, n), start=True, stop=True).then_inc(tt, 1)
                        if p == RGCN1:
                            pe.matmul(out, mat("root0"), X[:, col(h)], start=True, stop=True).then_inc(tt, 1)
                        if p == RGCN2:
                            pe.matmul(out, mat("root1"), H[:, col(h)], start=True, stop=True).then_inc(tt, 1)
                        if p == BASIS:
                            pe.matmul(out, mat("V0"), X[:, col(h)], start=True, stop=False)
                            pe.matmul(out, mat("V1"), acc[:, 0, col(h)], start=False, stop=False)
                            pe.matmul(out, mat("V2"), acc[:, 1, col(h)], start=False, stop=False)
                            pe.matmul(out, mat("loop"), X[:, col(h)], start=False, stop=True).then_inc(tt, 1)
                    if p in (GIN1, GIN2):
                        for h, o, n in hs:
                            after(a, aa, 1, "hidden", h)
                            pe.matmul(bank[4 + h][:, 0:n], mat("W1b" if p == GIN1 else "W2b"), part(1, h, n),
                                      start=True, stop=True).then_inc(tt, 1)
                    if p in NORMED:
                        for h, o, n in hs:
                            after(v, va, 0, "sum", h)
                            mb = 2 if p == GIN2 else 4
                            pe.matmul(bank[mb + h][:, 0:n], mean_m[:], part(2, h, n), start=True, stop=True).then_inc(tt, 1)
                        for h, o, n in hs:
                            after(a, aa, 1, "square", h)
                            pe.matmul(bank[6 + h][:, 0:n], mean_m[:], part(4, h, n), start=True, stop=True).then_inc(tt, 1)

                    def after_out(h):
                        if p in NORMED:
                            after(v, va, 0, "out", h)
                        else:
                            after(a, aa, 1, "outr", h)
                    if p in ROWS:
                        for h, o, n in hs:
                            after_out(h)
                            pe.wait_ge(s["rows_copied", h], i)
                            for k in range(n // P):
                                m = pe.transpose(bank[h][:, k * P:(k + 1) * P], part(5, h, n)[:, k * P:(k + 1) * P], ident[:])
                            m.then_inc(s["rows_ready", h], 1)
                    if p in WIDE:
                        for k in range(tails):
                            h = int(k * P >= hs[1][1])
                            if k * P == hs[h][1]:
                                after_out(h)
                            node = part(5, h, hs[h][2])[:, k * P - hs[h][1]:(k + 1) * P - hs[h][1]]
                            pe.wait_ge(s["lo_taken"], rows0 + k)
                            pe.matmul(bank[0][:], node, tw[:, 0:512], start=True, stop=True).then_inc(s["lo_ready"], 1)
                            pe.wait_ge(s["hi_taken"], rows0 + k)
                            pe.matmul(bank[1][:], node, tw[:, 512:1024], start=True, stop=True).then_inc(s["hi_ready"], 1)
                    if p in ROWS:
                        for h, o, n in hs:
                            pe.wait_ge(s["rows_copied", h], i + 1)
                    if p in WIDE:
                        pe.wait_ge(s["lo_taken"], rows0 + tails)
                        pe.wait_ge(s["hi_taken"], rows0 + tails)
                if p == RGCN1:
                    pe.wait_ge(tw_loaded, 16)

                def sweep_placed(sw):
                    placed[0] = pe.snap((sw + 1) * SETUP[p])

                def pass_placed():
                    placed[0] = pe.snap(needed * ((NSW + 1) * SETUP[p]))
                edge_pass(pe, p, needed, off, turn, node, setup=sweep_placed, main=pass_placed)
                pe.wait_ge(v, KV * NT)
                pe.wait_ge(a, KA * NT)

        @block.vector
        def _(dve):
            vec = nc.vector

            def tick0(ins, name):
                ins.then_inc(v0, 1)
                dve.wait_ge(v0, V0[name])
            dve.wait_ge(consts, 2)
            tick0(vec.tensor_copy(iota[:], iota_i[:]), "iota")
            tick0(vec.tensor_copy(pidx[:], pidx_i[:]), "pidx")
            tick0(vec.tensor_scalar(ident[:], iota[:], pidx[:, 0:1], None, ALU.is_equal), "ident")
            tick0(vec.memset(ones[:], 1.0), "ones")
            tick0(vec.memset(mean_m[:], 1.0 / D), "mean")
            dve.wait_ge(loaded, 16 * NLOAD)
            dq = work[0:QP, 0:2 * QUAD * P].bitcast(I32).rearrange("p (k e) -> p k e", k=2)
            dm = work[0:QP, 2 * QUAD * P:4 * QUAD * P].rearrange("p (k e) -> p k e", k=2)
            tick0(vec.tensor_reduce(bq[:], dq, AX.X, ALU.min), "qmin")
            tick0(vec.tensor_scalar(bq[:], bq[:], float(NP - W), None, ALU.min), "qcl")
            tick0(vec.scalar_tensor_tensor(dm, dq, float(NP), dq, ALU.is_lt, ALU.mult), "qmsk")
            tick0(vec.tensor_reduce(mq[:], dm, AX.X, ALU.max), "qmax")
            tick0(vec.tensor_tensor(mq[:], mq[:], bq[:], ALU.subtract), "qspan")
            tick0(vec.tensor_reduce(wq[:], mq[:], AX.X, ALU.max), "qwide")
            dve.wait_ge(t0, T0["vv"])
            tick0(vec.tensor_copy(vv[:], bank[0][:, 0:3]), "vv")
            tick0(vec.tensor_scalar(v3b[:], ones[:], vv[:, 2:3], None, ALU.mult), "v3b")
            tick0(vec.tensor_scalar(u2b[:], ones[:], vv[:, 1:2], None, ALU.mult), "u2b")
            dve.wait_ge(t0, T0["c64"])
            tick0(vec.tensor_copy(c64[:], bank[1][:, 0:64]), "c64")
            dve.wait_ge(t0, T0["pcol"])
            tick0(vec.tensor_copy(pcol[:], bank[4][:, 0:NP // P]), "pcol")
            dve.wait_ge(based_back, 32)
            tick0(vec.tensor_reduce(chk[:, 0:1], wide[:], AX.X, ALU.max), "spans")
            tick0(vec.tensor_scalar(chk[:, 0:1], chk[:, 0:1], float(W), None, ALU.is_ge), "wide")
            for j in range(NT - 1):
                turns, end = (LAG + (j + 1) * C, (j + 1) * TURN) if j < FULL else (NB - 1, NP - last)
                tick0(vec.tensor_reduce(chk[:, j + 1:j + 2], base_keep[:, turns * QT:], AX.X, ALU.min), f"late{j}a")
                tick0(vec.tensor_scalar(chk[:, j + 1:j + 2], chk[:, j + 1:j + 2], float(end), None, ALU.is_lt), f"late{j}b")
            tick0(vec.tensor_reduce(flag[:, 0:1], chk[:], AX.X, ALU.max), "flag")
            tick0(vec.tensor_scalar(flag[:, 1:2], flag[:, 0:1], -1.0e6, None, ALU.mult), "far")
            tick0(vec.tensor_scalar(flag[:, 2:3], flag[:, 0:1], -1.0, 1.0, ALU.mult, ALU.add), "keepf")
            tick0(vec.tensor_scalar(base_keep[:], base_keep[:], flag[:, 2:3], None, ALU.mult), "base_keep")
            tick0(vec.tensor_copy(flag_i[:], flag[0:1, 0:1]), "flag_i")

            def place(col, done, gat):
                done(vec.tensor_copy(base_i[:], base_keep[0:1, :]) if col == 1 else
                     vec.tensor_scalar(base_i[:], base_keep[0:1, :], flag[0:1, col:col + 1], None, ALU.add), "base_i")
                done(vec.tensor_scalar(base_f[:], base_keep[:], flag[:, col:col + 1], None, ALU.add), "base_f")
                done(vec.tensor_tensor(rel[:].rearrange("p (q c) -> p q c", c=QUAD),
                                       dst_i[:].rearrange("p (q c) -> p q c", c=QUAD),
                                       base_f[:].unsqueeze(2).broadcast_to([P, NQ, QUAD]), ALU.subtract), "rel")
                if gat:
                    done(vec.tensor_scalar(neg[:], rel[:], 0.0, None, ALU.is_ge), "neg1")
                    done(vec.scalar_tensor_tensor(w_edge[:], rel[:], float(W), neg[:], ALU.is_lt, ALU.mult), "neg2")
                    done(vec.tensor_scalar(neg[:], w_edge[:], 1.0, None, ALU.subtract), "neg3")
                    done(vec.tensor_scalar(neg[:], neg[:], BIG, None, ALU.mult), "neg4")
            place(1, tick0, True)
            tick0(vec.memset(flag[:, 3:4], 0.0), "off")
            tick0(vec.memset(Rmax[:], LOWEST), "R")
            tick0(vec.memset(eps[:], 1e-5), "eps")
            vec.memset(acc[:].rearrange("p a n -> p (a n)"), 0.0).then_inc(acc_zeroed, 1)
            dve.wait_ge(acc_zeroed, 1)
            needed, off = sweeping(dve)
            dve.wait_ge(a0, 2 * NT)

            def over_w(ap):
                return ap.unsqueeze(2).broadcast_to([P, G, W])
            iota_w = iota[:, 0:W].unsqueeze(1).broadcast_to([P, G, W])
            n_pre = 0
            for p in range(6):
                s = S[p]
                chain = s["chain"]

                def pre(ins):
                    nonlocal n_pre
                    ins.then_inc(prep, 1)
                    n_pre += 1
                    dve.wait_ge(prep, n_pre)

                def coefficients(b, dst, scratch):
                    for r in range(NREL):
                        cf = coef[:, 2 * r + b:2 * r + b + 1]
                        if r == 0:
                            pre(vec.tensor_scalar(dst[:], et8_i[:], float(r), cf, ALU.is_equal, ALU.mult))
                        else:
                            pre(vec.tensor_scalar(scratch[:], et8_i[:], float(r), cf, ALU.is_equal, ALU.mult))
                            pre(vec.tensor_tensor(dst[:], dst[:], scratch[:], ALU.add))
                if p:
                    dve.wait_ge(S[p - 1]["vn"], n_steps(p - 1, 0) * NT)
                if p == GIN1:
                    pre(vec.tensor_scalar(row_i[:], src_i[:], float(NREL), None, ALU.mult))
                    vec.tensor_tensor(row_i[:], row_i[:], et8_i[:], ALU.add).then_inc(rows_made, 1)
                if p == GIN2:
                    pre(vec.memset(w_edge[:], 0.0))
                if p == RGCN1:
                    pre(vec.tensor_scalar(w_edge[:], w_edge[:], 1.0, None, ALU.max))
                    pre(vec.reciprocal(w_edge[:], w_edge[:]))
                    pre(vec.memset(acc[:, 1, :], 0.0))
                if p == RGCN2:
                    coefficients(1, w_edge2, part_edges)
                if p == BASIS:
                    coefficients(0, w_edge, part_edges)

                def setup(sw):
                    base = dve.snap(sw * SETUP[p])
                    n = [0]

                    def done(ins, _):
                        ins.then_inc(s["setup"], 1)
                        n[0] += 1
                        dve.wait_ge(s["setup"], base + n[0])
                    place(3, done, p == GAT)
                    vec.tensor_scalar(flag[:, 3:4], flag[:, 3:4], float(W), None, ALU.add).then_inc(s["setup"], 1)
                    assert n[0] + 1 == SETUP[p]

                def restore():
                    n = [NSW * SETUP[p]]

                    def done(ins, _):
                        ins.then_inc(s["setup"], 1)
                        n[0] += 1
                        dve.wait_ge(s["setup"], n[0])
                    place(1, done, p == GAT)
                    done(vec.memset(flag[:, 3:4], 0.0), "")
                    assert n[0] == (NSW + 1) * SETUP[p]

                def add_group(k, T, t):
                    base = dve.snap((t * 2 + k) * SUMS[p])
                    f = windows(dve, T * 2 + k)
                    dve.wait_ge(s["chunk_done", k], t + 1)
                    if p == GAT:
                        dve.wait_ge(rescaled[k], t + 1)
                    n = 0
                    for q in range(GQ):
                        o = bank[k][:, q * 2 * W:(q + 1) * 2 * W]
                        win = bass.ds(f[q], W)
                        if q == 0:
                            dve.wait_ge(s["taken", 1 - k], t + k)
                        else:
                            dve.wait_ge(s["sums"], base + n)
                        if p == GIN1:
                            vec.tensor_tensor(acc[0:NREL, 1, win], acc[0:NREL, 1, win], o[0:NREL, W:2 * W], ALU.add).then_inc(s["sums"], 1)
                            n += 1
                        if p in (GAT, BASIS):
                            m = vec.tensor_tensor(acc[:, :, win], acc[:, :, win], o.rearrange("p (a w) -> p a w", a=2), ALU.add)
                        else:
                            m = vec.tensor_tensor(acc[:, 0, win], acc[:, 0, win], o[:, 0:W], ALU.add)
                        if q < GQ - 1:
                            m.then_inc(s["sums"], 1)
                            n += 1
                        elif p == GIN1:
                            m.then_inc(s["taken", k], 1)
                            dve.wait_ge(s["sums"], base + n)
                            dve.sem_inc(waited, 1)
                        else:
                            m.then_inc(s["taken", k], 1)
                    assert n == SUMS[p]

                def turn(T, t, first):
                    chain_base = dve.snap(t * CHAIN[p])
                    n_chain = 0

                    def step(ins):
                        nonlocal n_chain
                        ins.then_inc(chain, 1)
                        n_chain += 1

                    def settle():
                        dve.wait_ge(chain, chain_base + n_chain)
                    for k in range(2):
                        cols = bass.ds(T * (2 * G) + k * G, G)
                        hot = wo[k][:, 0, :, :]
                        f = windows(dve, T * 2 + k) if p == GAT else None
                        dve.wait_ge(s["weights_ready", 1 - k], t + k)
                        if p == GAT:
                            step(vec.tensor_tensor(oh, iota_w, over_w(rel[:, cols]), ALU.is_equal))
                            step(vec.tensor_tensor(logit[:, :, W:W + 64], iota[:, 0:64].unsqueeze(1).broadcast_to([P, G, 64]),
                                                   over_w(et64_i[:, cols]), ALU.is_equal))
                            step(vec.tensor_copy(logit[:, :, W + 64], neg[:, cols]))
                            settle()
                            for q in range(GQ):
                                qs = slice(q * QUAD, (q + 1) * QUAD)
                                step(vec.tensor_tensor(
                                    logit[:, qs, 0:W], oh[:, qs, :],
                                    H[:, bass.ds(f[q], W)].unsqueeze(1).broadcast_to([P, QUAD, W]), ALU.mult))
                            step(vec.tensor_tensor(logit[:, :, W:W + 64], logit[:, :, W:W + 64],
                                                   c64[:].unsqueeze(1).broadcast_to([P, G, 64]), ALU.mult))
                            settle()
                            step(vec.tensor_reduce(s_q[:], logit[:, :, 0:W + 65], AX.X, ALU.add))
                            if k == 1:
                                add_group(0, T, t)
                            elif not first:
                                add_group(1, T - 1, t - 1)
                            settle()
                            dve.wait_ge(gathering, t * 2 + (k + 1))
                            dve.sem_inc(waited, 1)
                            dve.wait_ge(landed[k], T * (16 * G) + 16 * G)
                            step(vec.tensor_tensor(att[:, k, :], s_q[:], msgs[k][:, :, D], ALU.add))
                            settle()
                            step(vec.scalar_tensor_tensor(att[:, k, :], att[:, k, :], 0.2, att[:, k, :], ALU.mult, ALU.max))
                            settle()
                            vec.tensor_reduce(gm[:, k:k + 1], att[:, k, :], AX.X, ALU.max).then_inc(gmax_part, 1)
                            dve.wait_ge(gmax_t, t * 2 + (k + 1))
                            vec.tensor_reduce(gx[0:1, k:k + 1], bank[2][0:1, 0:P], AX.X, ALU.max).then_inc(gmax_row, 1)
                            dve.wait_ge(gmax_all, t * 2 + (k + 1))
                            step(vec.tensor_tensor(Rmax[:, k:k + 1], Rmax[:, 1 - k:2 - k], bank[3][:, 0:1], ALU.max))
                            settle()
                            vec.tensor_scalar(nR[:, k:k + 1], Rmax[:, k:k + 1], -1.0, None, ALU.mult).then_inc(shift_ready, 1)
                            vec.tensor_tensor(dR[:, k:k + 1], Rmax[:, 1 - k:2 - k], Rmax[:, k:k + 1], ALU.subtract).then_inc(shift_ready, 1)
                            dve.wait_ge(exp_ready, t * 4 + (2 * k + 2))
                            vec.tensor_tensor(hot, oh, over_w(ex[:, k, :]), ALU.mult).then_inc(s["weights_ready", k], 1)
                        if p == GIN1:
                            step(vec.tensor_tensor(oe[k][:], iota[:, 0:NREL].unsqueeze(1).broadcast_to([P, G, NREL]),
                                                   et8_i[:, cols].unsqueeze(2).broadcast_to([P, G, NREL]), ALU.is_equal))
                            settle()
                            vec.tensor_tensor(hot, iota_w, over_w(rel[:, cols]), ALU.is_equal).then_inc(s["weights_ready", k], 1)
                        if p == GIN2:
                            vec.tensor_tensor(hot, iota_w, over_w(rel[:, cols]), ALU.is_equal).then_inc(s["weights_ready", k], 1)
                        if p in (RGCN1, RGCN2):
                            step(vec.tensor_tensor(oh, iota_w, over_w(rel[:, cols]), ALU.is_equal))
                            settle()
                            vec.tensor_tensor(hot, oh, over_w(w_edge[:, cols]), ALU.mult).then_inc(s["weights_ready", k], 1)
                        if p == BASIS:
                            step(vec.tensor_tensor(oh, iota_w, over_w(rel[:, cols]), ALU.is_equal))
                            settle()
                            step(vec.tensor_tensor(hot, oh, over_w(w_edge[:, cols]), ALU.mult))
                            settle()
                            vec.tensor_tensor(wo[k][:, 1, :, :], oh, over_w(w_edge2[:, cols]), ALU.mult).then_inc(s["weights_ready", k], 1)
                    if p != GAT:
                        for k in range(2):
                            if p == GIN2:
                                dve.wait_ge(types_loaded, t * 32 + (16 * (k + 1)))
                                vec.tensor_scalar(et_b, et_b.bitcast(I32), pidx[0:NREL, 0:1], None, ALU.is_equal).then_inc(types_hot, 1)
                            add_group(k, T, t)
                            if p == GIN2:
                                dve.wait_ge(picked, t * 2 + (k + 1))
                                own = wo[k][:, 0, :, :]
                                step(vec.tensor_tensor(tmp[:, 0:8, :], own[:, 0:8, :],
                                                       bank[4][:].rearrange("p (g w) -> p g w", g=8), ALU.mult))
                                vec.tensor_tensor(tmp[:, 8:16, :], own[:, 8:16, :],
                                                  bank[5][:].rearrange("p (g w) -> p g w", g=8), ALU.mult).then_inc(pick_taken, 1)
                                settle()
                                dve.wait_ge(pick_taken, t * 2 + (k + 1))
                                step(vec.tensor_reduce(s_q[:], tmp, AX.X, ALU.add))
                                settle()
                                cols = bass.ds(T * (2 * G) + k * G, G)
                                step(vec.tensor_tensor(w_edge[:, cols], w_edge[:, cols], s_q[:], ALU.add))
                    assert n_chain == CHAIN[p], (p, n_chain, CHAIN[p])

                def flush(T, t):
                    add_group(1, T, t)
                v, a, tt = s["vn"], s["an"], s["tn"]
                KV, KA, KT = (n_steps(p, e) for e in range(3))

                def node(i, t, *place):
                    hs, first, rows0, tails = tile(i, *place)
                    va, aa, ta = dve.snap(i * KV), dve.snap(i * KA), dve.snap(i * KT)
                    dve.wait_ge(s["taken", 1], t)

                    def after(sm, base, e, name, h):
                        dve.wait_ge(sm, base + step_at(p, e, name, h))

                    def col(h):
                        return bass.ds(first + hs[h][1], hs[h][2])
                    if p == GAT:
                        for h, o, n in hs:
                            dve.wait_ge(tt, ta)
                            dve.wait_ge(a, aa)
                            vec.tensor_scalar(part(1, h, n), acc[:, 1, col(h)], 1e-10, None, ALU.add).then_inc(v, 1)
                        for h, o, n in hs:
                            after(v, va, 0, "guard", h)
                            vec.reciprocal(part(4, h, n), part(1, h, n)).then_inc(v, 1)
                        for h, o, n in hs:
                            after(v, va, 0, "recip", h)
                            vec.tensor_tensor(part(0, h, n), acc[:, 0, col(h)], part(4, h, n), ALU.mult).then_inc(v, 1)
                        for h, o, n in hs:
                            after(tt, ta, 2, "lin", h)
                            vec.tensor_tensor(part(2, h, n), bank[2 + h][:, 0:n], X[:, col(h)], ALU.add).then_inc(v, 1)
                    if p in (GIN1, GIN2):
                        for h, o, n in hs:
                            dve.wait_ge(tt, ta)
                            dve.wait_ge(a, aa)
                            vec.tensor_tensor(part(0, h, n), acc[:, 0, col(h)], (X if p == GIN1 else H)[:, col(h)], ALU.add).then_inc(v, 1)
                    if p == GIN1:
                        for h, o, n in hs:
                            after(a, aa, 1, "outr", h)
                            vec.tensor_copy(H[:, col(h)], part(5, h, n)).then_inc(v, 1)
                    if p == GIN2:
                        for h, o, n in hs:
                            after(tt, ta, 2, "lin2", h)
                            vec.scalar_tensor_tensor(part(2, h, n), bank[4 + h][:, 0:n], bcol("b2b"), X[:, col(h)],
                                                     ALU.add, ALU.add).then_inc(v, 1)
                    if p == RGCN1:
                        for h, o, n in hs:
                            after(tt, ta, 2, "lin", h)
                            dve.wait_ge(a, aa)
                            vec.tensor_tensor(part(2, h, n), bank[2 + h][:, 0:n], acc[:, 0, col(h)], ALU.add).then_inc(v, 1)
                        for h, o, n in hs:
                            after(a, aa, 1, "outr", h)
                            vec.tensor_copy(H[:, col(h)], part(5, h, n)).then_inc(v, 1)
                    if p == RGCN2:
                        for h, o, n in hs:
                            after(tt, ta, 2, "lin", h)
                            vec.tensor_tensor(part(0, h, n), bank[2 + h][:, 0:n], acc[:, 0, col(h)], ALU.add).then_inc(v, 1)
                        for h, o, n in hs:
                            after(v, va, 0, "sum0", h)
                            vec.scalar_tensor_tensor(part(2, h, n), part(0, h, n), bcol("bias1"), X[:, col(h)], ALU.add, ALU.add).then_inc(v, 1)
                    if p == BASIS:
                        for h, o, n in hs:
                            after(tt, ta, 2, "lin", h)
                            vec.scalar_tensor_tensor(part(2, h, n), bank[2 + h][:, 0:n], bcol("h_bias"), X[:, col(h)],
                                                     ALU.add, ALU.add).then_inc(v, 1)
                    if p in NORMED:
                        mb = 2 if p == GIN2 else 4
                        for h, o, n in hs:
                            after(tt, ta, 2, "mean", h)
                            after(v, va, 0, "sum", h)
                            vec.tensor_tensor(part(3, h, n), part(2, h, n), bank[mb + h][:, 0:n], ALU.subtract).then_inc(v, 1)
                        for h, o, n in hs:
                            after(a, aa, 1, "std", h)
                            vec.reciprocal(part(0, h, n), part(1, h, n)).then_inc(v, 1)
                        for h, o, n in hs:
                            after(v, va, 0, "rstd", h)
                            if p in ROWS:
                                dve.wait_ge(s["rows_ready", h], i)
                            if p in WIDE:
                                dve.wait_ge(s["hi_ready"], rows0)
                            if p == BASIS:
                                dve.wait_ge(out_stored[h], i * 16)
                            vec.tensor_tensor(part(5, h, n), part(3, h, n), part(0, h, n), ALU.mult).then_inc(v, 1)
                    if p != BASIS:
                        both = acc[:] if p == GAT else acc[:, 0:1, :]
                        for h, o, n in hs:
                            block = both[:, :, col(h)]
                            vec.tensor_scalar(block, block, 0.0, None, ALU.mult).then_inc(v, 1)
                    if p in WIDE:
                        for k in range(tails):
                            dve.wait_ge(s["hi_ready"], rows0 + (k + 1))
                            b, stored = slot(i, k, *place)
                            dve.wait_ge(s["wide_stored", b], stored)
                            vec.tensor_copy(stage[b][:, 512:1024], bank[1][:]).then_inc(s["hi_taken"], 1)
                    dve.wait_ge(v, va + KV)
                edge_pass(dve, p, needed, off, turn, node, setup, restore, flush if p == GAT else None)


INS = ["x_rows", "xT", "src_pt", "dst_pt", "dst_q", "et64_pt", "et8_pt", "et8_flat", "mats", "bias", "avec", "relT",
       "tw0", "tw1", "coeff"]


def lay_out(x, src, dst, edge_type_64, edge_type_8, w):
    N, E = x.shape[0], src.shape[0]
    NP, NCH = sizes(N, E)

    def padded(a, fill):
        return np.concatenate([a, np.full(NCH * P - E, fill, a.dtype)])

    def pt(a):
        return np.ascontiguousarray(a.reshape(NCH, P).T)
    d, e8 = padded(dst, 4 * NP), padded(edge_type_8, 0)
    return {
        "x_rows": np.concatenate([x, np.zeros((NP - N, D), x.dtype)]),
        "xT": np.ascontiguousarray(np.concatenate([x, np.zeros((NP - N, D), x.dtype)]).T),
        "src_pt": pt(padded(src, 0)), "dst_pt": pt(d), "dst_q": d.reshape(NCH // QUAD // 2, 2 * QUAD * P),
        "et64_pt": pt(padded(edge_type_64, 0)), "et8_pt": pt(e8), "et8_flat": e8.reshape(1, -1),
        "mats": np.concatenate([w["L0_gnn_W"], w["L1_gnn_W1a"], w["L1_gnn_W1b"], w["L1_gnn_W2a"], w["L1_gnn_W2b"],
                                w["L2_gnn_roots"][0], w["L2_gnn_roots"][1], w["L3_gnn_W"][0], w["L3_gnn_W"][1],
                                w["L3_gnn_W"][2], w["L3_gnn_loop_weight"], w["L0_gnn_W"].T, w["L0_gnn_W_r"].T], axis=1),
        "bias": np.stack([w["L1_gnn_b1a"], w["L1_gnn_b1b"], w["L1_gnn_b2a"], w["L1_gnn_b2b"], w["L2_gnn_biases"][0],
                          w["L2_gnn_biases"][1], w["L3_gnn_h_bias"]], axis=1),
        "avec": np.ascontiguousarray(w["L0_gnn_a"].reshape(3, D).T),
        "relT": np.ascontiguousarray(w["L0_gnn_rel_emb"].T),
        "tw0": np.concatenate(list(w["L2_gnn_weights"][0]), axis=1),
        "tw1": np.concatenate(list(w["L2_gnn_weights"][1]), axis=1),
        "coeff": np.ascontiguousarray(w["L3_gnn_coeff"].reshape(1, -1)),
    }


def kernel(x, src, dst, edge_type_64, edge_type_8, **weights):
    import concourse.bacc as bacc
    from concourse.bass_utils import run_bass_kernel_spmd

    x, src, dst, e64, e8 = (np.asarray(a) for a in (x, src, dst, edge_type_64, edge_type_8))
    N, E = x.shape[0], src.shape[0]
    arrays = lay_out(x, src, dst, e64, e8, {k: np.asarray(v) for k, v in weights.items()})
    nc = bacc.Bacc("TRN2", target_bir_lowering=False, num_devices=1)
    args = [nc.dram_tensor(n, arrays[n].shape, mybir.dt.from_np(arrays[n].dtype), kind="ExternalInput").ap() for n in INS]
    outT = nc.dram_tensor("outT", [P, sizes(N, E)[0]], F32, kind="ExternalOutput").ap()
    with nc.allow_non_contiguous_dma("columns of small arrays"):
        build(nc, N, E, *args, outT)
    r = run_bass_kernel_spmd(nc, [arrays], core_ids=[0])
    return np.ascontiguousarray(r.results[0]["outT"][:, :N].T)
```

```python
import numpy as np
import concourse.bass as bass
from concourse import mybir

F32 = mybir.dt.float32
I32 = mybir.dt.int32
BF16 = mybir.dt.bfloat16
ALU = mybir.AluOpType
ACT = mybir.ActivationFunctionType
AX = mybir.AxisListType

P = 128
D = 128
W = 64
QUAD = 4
G = 16
GQ = G // QUAD
TURN = 4 * P
NREL = 8
SETS = 64 + NREL
BIG = 1.0e30
LOWEST = -3.0e38


def round_up(a, b):
    return (a + b - 1) // b * b


def sizes(n_nodes, n_edges):
    return round_up(n_nodes, P), round_up(-(-n_edges // P), 2 * G)


MATS = ["W", "W1a", "W1b", "W2a", "W2b", "root0", "root1", "V0", "V1", "V2", "loop", "WT", "WrT"]
BIAS = ["b1a", "b1b", "b2a", "b2b", "bias0", "bias1", "h_bias"]

GAT, GIN1, GIN2, RGCN1, RGCN2, BASIS = range(6)
FRONT = {
    GAT: (["norm", "sum"], [], ["den", "lin"]),
    GIN1: (["zin", "hi", "rest", "mid", "low", "midrows", "lowrows", "keep"], ["hidden", "outr"], ["counts", "lin", "lin2"]),
    GIN2: (["zin", "sum"], ["hidden"], ["lin", "lin2"]),
    RGCN1: (["sum", "keep"], ["outr"], ["lin"]),
    RGCN2: (["sum0", "sum"], [], ["lin"]),
    BASIS: (["sum"], [], ["lin"]),
}
EXTRA = {GAT: 1, GIN1: NREL}
NORMED = (GAT, GIN2, RGCN2, BASIS)
ROWS = (GAT, GIN1, RGCN2)
WIDE = (GIN2, RGCN1)


def steps_of(p):
    v, a, t = (list(x) for x in FRONT[p])
    if p in NORMED:
        v += ["center", "rstd", "out"]
        a += ["square", "std", "store"]
        t += ["mean", "var"]
    if p != BASIS:
        v += ["zero"]
    return v, a, t


def build(nc, N, E, x_rows, xT, src_pt, dst_pt, dst_q, et64_pt, et8_pt, et8_flat, mats, bias, avec, relT, tw0, tw1,
          coeff, outT):
    NP, NCH = sizes(N, E)
    NQ = NCH // QUAD
    QP = NQ // 2
    NB = NCH // (2 * G)
    FULL = (NP - 3 * P - 1) // TURN
    rest = NP - FULL * TURN
    last = 3 * P if rest >= 5 * P else 2 * P
    NT = FULL + 2
    TAIL_TILES = [(FULL, FULL * TURN, rest - last), (FULL + 1, NP - last, last)]
    NSW = NP // W
    BIG_TURN = 2 * TURN
    BIG_FULL = NP // BIG_TURN - 1
    rest = NP - BIG_FULL * BIG_TURN
    big_first = round_up(rest // 2, P)
    BIG_TAIL_TILES = [(BIG_FULL, BIG_FULL * BIG_TURN, big_first), (BIG_FULL + 1, NP - rest + big_first, rest - big_first)]
    TILES = {p: BIG_FULL + 2 if p == GAT else NT for p in range(6)}
    C = min(max(1, TURN * E // (N * 2 * G * P)), (NB - 1) // FULL)
    LAG = max(0, min(-(-FULL * TURN * E // (N * 2 * G * P)) - (FULL - 1) * C - 1, NB - 1 - FULL * C))
    QT = 2 * GQ
    from contextlib import ExitStack
    ctx = ExitStack()
    with ctx:
        def sb(name, shape, dt=F32):
            return ctx.enter_context(nc.sbuf_tensor(name, shape, dt))

        def sem(name):
            return ctx.enter_context(nc.semaphore(name))

        def dram(name, shape, dt=F32):
            return nc.dram_tensor(name, shape, dt, kind="Internal").ap()

        table0 = dram("table0", [NP, D + 1])
        table_gin1 = dram("table_gin1", [NP, D])
        table_gin2 = dram("table_gin2", [NP, D])
        table_rel1 = dram("table_rel1", [NP * NREL, D])
        table_rel2 = dram("table_rel2", [NP * NREL, D])
        table_basis = dram("table_basis", [NP, D])
        base_d = dram("base_d", [1, NQ])
        den_d = dram("den_d", [1, NP])
        inverse_d = dram("inverse_d", [1, NP])
        wide_d = dram("wide_d", [1, QP])
        tables = {GAT: table0, GIN1: table_gin1, GIN2: table_gin2, RGCN1: table_rel1, RGCN2: table_rel2,
                  BASIS: table_basis}
        next_table = {GAT: table_gin1, GIN1: table_gin2, GIN2: table_rel1, RGCN1: table_rel2, RGCN2: table_basis}

        acc = sb("acc", [P, 2, NP])
        X = sb("X", [P, NP])
        H = sb("H", [P, NP])
        msgs = [sb(f"msgs{k}", [P, G, D + 1]) for k in range(2)]
        wo = [sb(f"wo{k}", [P, 2, G, W]) for k in range(2)]
        idx = [sb(f"idx{k}", [P, G], I32) for k in range(2)]
        work = sb("work", [P, 3 * G * W + 3 * G * P // 2])
        src_i = sb("src_i", [P, NCH], I32)
        dst_i = sb("dst_i", [P, NCH], I32)
        et64_i = sb("et64_i", [P, NCH], I32)
        row_i = et64_i
        et8_i = sb("et8_i", [P, NCH], I32)
        rel = sb("rel", [P, NCH])
        w_edge = sb("w_edge", [P, NCH])
        w_edge2 = sb("w_edge2", [P, NCH])
        neg = w_edge2
        base_keep = sb("base_keep", [P, NQ])
        base_f = sb("base_f", [P, NQ])
        base_i = sb("base_i", [1, NQ], I32)
        wide = sb("wide", [P, QP])
        chk = sb("chk", [P, NT])
        flag = sb("flag", [P, 4])
        flag_i = sb("flag_i", [1, 1], I32)
        bq = sb("bq", [QP, 2])
        mq = sb("mq", [QP, 2])
        wq = sb("wq", [QP, 1])
        m_sb = sb("m_sb", [P, len(MATS), D])
        b_sb = sb("b_sb", [P, len(BIAS)])
        a_sb = sb("a_sb", [P, 3])
        relT_sb = sb("relT_sb", [P, 64])
        tw = sb("tw", [P, NREL * D])
        coef = sb("coef", [P, NREL * 2])
        vv = sb("vv", [P, 3])
        v3b = sb("v3b", [P, P])
        u2b = sb("u2b", [P, P])
        den = sb("den", [P, NP // P])
        c64 = sb("c64", [P, 64])
        pcol = sb("pcol", [P, NP // P])
        iota_i = sb("iota_i", [P, P], I32)
        iota = sb("iota", [P, P])
        pidx_i = sb("pidx_i", [P, 1], I32)
        pidx = sb("pidx", [P, 1])
        in_set = sb("in_set", [P, 1])
        spread = sb("spread", [NREL, SETS])
        ident = sb("ident", [P, P])
        ones = sb("ones", [P, P])
        mean_m = sb("mean_m", [P, P])
        oe = [sb(f"oe{k}", [P, G, NREL]) for k in range(2)]
        s_q = sb("s_q", [P, G])
        s_c = sb("s_c", [P, G])
        att = sb("att", [P, 2, G])
        ex = sb("ex", [P, 2, G])
        gm = sb("gm", [P, 2])
        gx = sb("gx", [1, 2])
        Rmax = sb("Rmax", [P, 2])
        dR = sb("dR", [P, 2])
        nR = sb("nR", [P, 2])
        rose = sb("rose", [1, 2], I32)
        alpha = sb("alpha", [P, 2])
        stage = [sb(f"stage{k}", [P, NREL * D])[:, :] for k in range(2)]
        stage += [wo[k][:, 1, :, :].rearrange("p g w -> p (g w)") for k in range(2)]
        eps = sb("eps", [P, 1])

        oh = work[:, 0:G * W].rearrange("p (g w) -> p g w", g=G)
        tmp = work[:, G * W:2 * G * W].rearrange("p (g w) -> p g w", g=G)
        LG = W + 64 + 2
        logit = work[:, G * W:G * W + G * LG].rearrange("p (g w) -> p g w", g=G)
        assert 6 * BIG_TURN <= 3 * G * W + 3 * G * P // 2
        assert 6 * TURN <= 3 * G * W
        part_edges = work[:, 0:NCH]
        types = work[0:SETS, 3 * G * W:3 * G * W + G * P].bitcast(I32)
        types_b = work[0:SETS, 3 * G * W + G * P:3 * G * W + 3 * G * P // 2].bitcast(BF16)
        counts = acc[0:SETS, 1, :].bitcast(BF16).rearrange("p (n two) -> p n two", two=2)[:, :, 0]

        def tile(i, first=None, n=None, turn=TURN):
            n = n or turn
            half = -(-n // (2 * P)) * P
            rows0 = i * (turn // P) if first is None else first // P
            return [(0, 0, half), (1, half, n - half)], i * turn if first is None else first, rows0, n // P

        def slot(i, k, first=None, n=TURN):
            if first is None:
                return k, i * 16
            return (first // P + k) % 4, 16 * ((first // P + k) // 4)

        def temporaries(p):
            half = (BIG_TURN if p == GAT else TURN) // 2
            return lambda k, h, n: work[:, (2 * k + h) * half:(2 * k + h) * half + n]
        bank = [ctx.enter_context(nc.psum_tensor(f"bank{k}", [P, 512], F32)) for k in range(8)]

        def mat(name):
            return m_sb[:, MATS.index(name), :]

        def bcol(name):
            k = BIAS.index(name)
            return b_sb[:, k:k + 1]

        loaded = sem("loaded")
        idx_ready = [sem(f"idx_ready{k}") for k in range(2)]
        landed = [sem(f"landed{k}") for k in range(2)]
        prep = sem("prep")
        gathering = sem("gathering")
        den_moved = sem("den_moved")
        den_inverted = sem("den_inverted")
        waited = sem("waited")
        emptied = sem("emptied")
        used_up = sem("used_up")
        x_copied = sem("x_copied")
        pcol_out = sem("pcol_out")
        consts = sem("consts")
        v0 = sem("v0")
        a0 = sem("a0")
        t0 = sem("t0")
        based = sem("based")
        based_back = sem("based_back")
        S = [dict() for _ in range(6)]
        for p in range(6):
            for k in range(2):
                for n in ( "weights_ready", "chunk_done", "taken"):
                    S[p][n, k] = sem(f"{n}{k}_{p}")
                if p in ROWS:
                    for n in ("rows_ready", "rows_copied", "rows_stored"):
                        S[p][n, k] = sem(f"{n}{k}_{p}")
            for n in ("setup", "chain", "sums", "vn", "an", "tn"):
                S[p][n] = sem(f"{n}_{p}")
            if p in WIDE:
                for n in ("lo_ready", "hi_ready", "lo_taken", "hi_taken"):
                    S[p][n] = sem(f"{n}_{p}")
                for k in range(4):
                    S[p]["wide_stored", k] = sem(f"wide_stored{k}_{p}")
        gmax_part, gmax_t, gmax_row, gmax_all, shift_ready, exp_ready = (
            sem(n) for n in ("gmax_part", "gmax_t", "gmax_row", "gmax_all", "shift_ready", "exp_ready"))
        rescaled = [sem(f"rescaled{k}") for k in range(2)]
        types_loaded, types_hot, picked, pick_taken = (
            sem(n) for n in ("types_loaded", "types_hot", "picked", "pick_taken"))
        rows_made = sem("rows_made")
        acc_zeroed = sem("acc_zeroed")
        tw_loaded = sem("tw_loaded")
        out_stored = [sem(f"out_stored{h}") for h in range(2)]

        NLOAD = 13
        block = ctx.enter_context(nc.Block())

        def sweeping(eng):
            eng.wait_ge(v0, V0["flag_i"])
            f = eng.value_load(flag_i[0:1, 0:1], min_val=0, max_val=1)
            return f, eng.snap(f * (NSW * NB))

        def windows(eng, group):
            _, first = nc.values_load_multi_w_load_instructions(
                base_i[0:1, bass.ds(group * GQ, GQ)], engines=(eng.engine,), min_val=0, max_val=NP - W,
                skip_runtime_bounds_check_because="VectorE clamps them to 0 .. NP - W")
            return first

        def edge_pass(eng, p, needed, off, turn, node, setup=None, restore=None, flush=None,
                      main=None, begin=None, end=None, between=None):
            def run(lo, hi, before):
                if begin:
                    begin(before)
                if flush is None:
                    with eng.Fori(lo, hi) as T:
                        turn(T, eng.snap(before + T), False)
                    if end and hi == NB:
                        end(hi - 1, eng.snap(before + (hi - 1)))
                    return
                turn(lo, eng.snap(before + lo), True)
                if hi > lo + 1:
                    with eng.Fori(lo + 1, hi) as T:
                        turn(T, eng.snap(before + T), False)
                flush(hi - 1, eng.snap(before + (hi - 1)))
            with eng.If(needed > 0):
                with eng.Fori(0, NSW) as sw:
                    if setup:
                        setup(sw)
                    run(0, NB, eng.snap(sw * NB))
                if restore:
                    restore()
            if main:
                main()
            if p == GAT:
                run(0, NB, off)
                if between:
                    between()
                if BIG_FULL:
                    with eng.Fori(0, BIG_FULL) as j:
                        for step in node:
                            step(j, eng.snap(off + NB))
                for n_tile in BIG_TAIL_TILES:
                    for step in node:
                        step(n_tile[0], eng.snap(off + NB), *n_tile[1:])
                return
            if begin:
                begin(off)
            if LAG:
                with eng.Fori(0, LAG) as T:
                    turn(T, eng.snap(off + T), False)
            with eng.Fori(0, FULL) as j:
                first = eng.snap(j * C + LAG)
                for u in range(C):
                    T = eng.snap(first + u)
                    turn(T, eng.snap(off + T), False)
                    for step in node[:1] if u == 0 else ():
                        step(j, eng.snap(off + first + 1))
                for step in node[1:]:
                    step(j, eng.snap(off + first + C))
            if FULL * C + LAG < NB - 1:
                with eng.Fori(FULL * C + LAG, NB - 1) as T:
                    turn(T, eng.snap(off + T), False)
            for step in node:
                step(TAIL_TILES[0][0], eng.snap(off + (NB - 1)), *TAIL_TILES[0][1:])
            run(NB - 1, NB, off)
            for step in node:
                step(TAIL_TILES[1][0], eng.snap(off + NB), *TAIL_TILES[1][1:])

        def n_steps(p, e):
            return 2 * len(steps_of(p)[e])

        def step_at(p, e, name, h):
            return 2 * steps_of(p)[e].index(name) + h + 1

        V0 = {n: k + 1 for k, n in enumerate(
            ["iota", "pidx", "ident", "ones", "mean", "set1", "set2", "set3", "set4", "spread0", "spread1", "spread2", "spread3", "qmin", "qcl", "qmsk", "qmax", "qspan", "qwide", "vv", "v3b", "u2b",
             "spans", "wide"] + [f"late{j}{x}" for j in range(NT - 1) for x in "ab"] +
            ["flag", "far", "keepf", "base_keep", "flag_i", "c64", "pcol", "base_i", "base_f", "rel", "neg1", "neg2", "neg3", "neg4",
             "off", "R", "eps"])}
        T0 = {n: k + 1 for k, n in enumerate(["vv", "c64", "pcol"])}
        TQ = len(T0)
        SETUP = {p: (8 if p == GAT else 4) for p in range(6)}
        CHAIN = {GAT: 2 * 12, GIN1: 2, GIN2: 2 * 3, RGCN1: 2, RGCN2: 2, BASIS: 2 * 2}
        SUMS = {p: GQ - 1 + (GQ if p in EXTRA else 0) for p in range(6)}
        TAILS = TURN // P
        TAILS_IN_ALL = NP // P

        @block.sync
        def _(sp):
            for dst, src in ((X[:], xT), (src_i[:], src_pt), (dst_i[:], dst_pt), (et64_i[:], et64_pt),
                             (et8_i[:], et8_pt), (m_sb[:], mats.rearrange("p (k d) -> p k d", d=D)), (b_sb[:], bias),
                             (a_sb[:], avec), (relT_sb[:], relT), (tw[:], tw0),
                             (coef[:], coeff.to_broadcast([P, NREL * 2])),
                             (work[0:QP, 0:2 * QUAD * P].bitcast(I32), dst_q)):
                sp.dma_start(dst, src).then_inc(loaded, 16)
            sp.dma_start(work[0:1, 4 * QUAD * P:4 * QUAD * P + 16], mats[0:1, 0:16]).then_inc(loaded, 16)
            sp.wait_ge(v0, V0["qwide"])
            sp.dma_start(base_d.rearrange("o (p k) -> (o p) k", k=2), bq[:]).then_inc(based, 16)
            sp.dma_start(wide_d.rearrange("o p -> p o"), wq[:]).then_inc(based, 16)
            sp.wait_ge(based, 32)
            sp.dma_start(base_keep[:], base_d.to_broadcast([P, NQ])).then_inc(based_back, 16)
            sp.dma_start(wide[:], wide_d.to_broadcast([P, QP])).then_inc(based_back, 16)
            sp.wait_ge(v0, V0["pcol"])
            sp.dma_start(table0.rearrange("(t p) c -> p t c", p=P)[:, :, D:D + 1],
                         pcol[:].unsqueeze(2)).then_inc(pcol_out, 16)
            needed, off = sweeping(sp)
            for p in range(6):
                s = S[p]
                rows = row_i if p in (RGCN1, RGCN2) else src_i
                if p == RGCN1:
                    sp.wait_ge(rows_made, 1)
                    sp.wait_ge(S[GIN2]["hi_ready"], TAILS_IN_ALL)
                    sp.dma_start(tw[:], tw1).then_inc(tw_loaded, 16)

                if p:
                    for k in range(2):
                        sp.wait_ge(S[p - 1]["chunk_done", k], off + NB)
                    sp.sem_inc(waited, 1)

                def turn(T, t, _):
                    for k in range(2):
                        sp.wait_ge(s["chunk_done", k], t)
                        sp.dma_start(idx[k][:], rows[:, bass.ds(T * (2 * G) + k * G, G)]).then_inc(idx_ready[k], 16)
                        if p == GIN2:
                            sp.wait_ge(types_hot, t * 2 + k)
                            for first in (0, 32, 64):
                                sp.dma_start(types[first:first + NREL, :],
                                             et8_flat[0:1, bass.ds(T * (2 * G * P) + k * G * P, G * P)].to_broadcast(
                                                 [NREL, G * P])).then_inc(types_loaded, 16)

                if p == GIN2:
                    sp.wait_ge(rows_made, 2)
                edge_pass(sp, p, needed, off, turn, ())
                if p == GAT:
                    for k in range(2):
                        sp.wait_ge(s["taken", k], off + NB)
                    sp.sem_inc(waited, 1)
                    sp.wait_ge(s["sums"], (off + NB) * (2 * SUMS[p]))
                    sp.dma_start(den_d, acc[0:1, 1, :]).then_inc(den_moved, 16)
                    sp.wait_ge(den_moved, 16)
                    sp.dma_start(den[:], den_d.rearrange("o (p k) -> (o p) k", p=P)).then_inc(den_moved, 16)
                    sp.wait_ge(den_inverted, 2)
                    sp.dma_start(inverse_d.rearrange("o (p k) -> (o p) k", p=P), den[:]).then_inc(den_moved, 16)
                    sp.wait_ge(den_moved, 48)
                    sp.dma_start(acc[0:1, 1, :], inverse_d).then_inc(den_moved, 16)
            for h in range(2):
                sp.wait_ge(out_stored[h], 16 * NT)

        @block.gpsimd
        def _(pool):
            pool.dma_start(table0[:, 0:D], x_rows).then_inc(x_copied, 16)
            pool.iota(iota_i[:], pattern=[[1, P]], base=0, channel_multiplier=0).then_inc(consts, 1)
            pool.iota(pidx_i[:], pattern=[[0, 1]], base=0, channel_multiplier=1).then_inc(consts, 1)
            pool.wait_ge(x_copied, 16)
            pool.wait_ge(pcol_out, 16)
            needed, off = sweeping(pool)
            for p in range(6):
                s = S[p]
                if p and p - 1 in ROWS:
                    for h in range(2):
                        pool.wait_ge(S[p - 1]["rows_stored", h], 16 * TILES[p - 1])
                if p and p - 1 in WIDE:
                    for k in range(4):
                        pool.wait_ge(S[p - 1]["wide_stored", k], 16 * len(range(k, TAILS_IN_ALL, 4)))
                width = D + 1 if p == GAT else D

                def turn(T, t, _):
                    for k in range(2):
                        pool.wait_ge(idx_ready[k], (off + NB) * (16 * p) + t * 16 + 16)
                        pool.wait_ge(s["chunk_done", k], t)
                        pool.wait_ge(emptied, (off + NB) * p + swept[0])
                        pool.sem_inc(gathering, 1)
                        for c in range(G):
                            pool.indirect_dma_start(
                                out=msgs[k][:, c, 0:width], out_offset=None, in_=tables[p],
                                in_offset=bass.IndirectOffsetOnAxis(ap=idx[k][:, c:c + 1], axis=0)).then_inc(
                                    landed[k], 16)
                def settled(_, t):
                    for k in range(2):
                        pool.wait_ge(s["chunk_done", k], t + 1)
                    pool.sem_inc(used_up, 1)
                    pool.inc_swdge_sem(landed, [16 * G * NB] * 2, mode="sub").then_inc(emptied, NB)
                swept = [0]

                def begin(before):
                    swept[0] = before
                edge_pass(pool, p, needed, off, turn, (), begin=begin, end=settled)

        @block.scalar
        def _(act):
            def q_out(i, *place):
                hs, first, _, _ = tile(i, *place, turn=BIG_TURN)
                for h, o, n in hs:
                    act.wait_ge(t0, i * 2 + (TQ + h + 1))
                    nc.scalar.activation(H[:, bass.ds(first + o, n)], bank[2 + h][:, 0:n], ACT.Copy).then_inc(a0, 1)
            if BIG_FULL:
                with act.Fori(0, BIG_FULL) as i:
                    q_out(i)
            for n_tile in BIG_TAIL_TILES:
                q_out(*n_tile)
            needed, off = sweeping(act)
            for p in range(6):
                s = S[p]
                v, a, tt = s["vn"], s["an"], s["tn"]
                part = temporaries(p)
                KV, KA, KT = (n_steps(p, e) for e in range(3))

                def turn(T, t, _):
                    for k in range(2):
                        act.wait_ge(shift_ready, t * 6 + (3 * k + 3))
                        nc.scalar.activation(alpha[:, k:k + 1], dR[:, k:k + 1], ACT.Exp).then_inc(exp_ready, 1)
                        nc.scalar.activation(ex[:, k, :], att[:, k, :], ACT.Exp, bias=nR[:, k:k + 1]).then_inc(exp_ready, 1)
                        f = act.value_load(rose[0:1, k:k + 1], min_val=0, max_val=1)
                        with act.If(f > 0):
                            act.wait_ge(exp_ready, t * 4 + (2 * k + 1))
                            act.sem_inc(waited, 1)
                            act.wait_ge(s["taken", 1 - k], t + k)
                            flat = acc[:].rearrange("p a n -> p (a n)")
                            nc.scalar.activation(flat, flat, ACT.Copy, scale=alpha[:, k:k + 1]).then_inc(rescaled[k], 1)
                        with act.If(f < 1):
                            act.sem_inc(rescaled[k], 1)

                def node(i, t, *place):
                    hs, first, rows0, tails = tile(i, *place, turn=BIG_TURN if p == GAT else TURN)
                    va, aa, ta = act.snap(i * KV), act.snap(i * KA), act.snap(i * KT)

                    def after(sm, base, e, name, h):
                        act.wait_ge(sm, base + step_at(p, e, name, h))

                    def col(h):
                        return bass.ds(first + hs[h][1], hs[h][2])
                    if p in (GIN1, GIN2):
                        for h, o, n in hs:
                            after(tt, ta, 2, "lin", h)
                            nc.scalar.activation(part(1, h, n), bank[2 + h][:, 0:n], ACT.Relu,
                                                 bias=bcol("b1a" if p == GIN1 else "b2a")).then_inc(a, 1)
                    if p == GIN1:
                        for h, o, n in hs:
                            after(tt, ta, 2, "lin2", h)
                            act.wait_ge(v, va)
                            act.wait_ge(s["rows_ready", h], i)
                            nc.scalar.activation(part(5, h, n), bank[4 + h][:, 0:n], ACT.Relu, bias=bcol("b1b")).then_inc(a, 1)
                    if p == RGCN1:
                        for h, o, n in hs:
                            after(v, va, 0, "sum", h)
                            act.wait_ge(s["hi_ready"], rows0)
                            nc.scalar.activation(part(5, h, n), part(2, h, n), ACT.Relu, bias=bcol("bias0")).then_inc(a, 1)
                    if p in NORMED:
                        for h, o, n in hs:
                            after(v, va, 0, "center", h)
                            nc.scalar.activation(part(4, h, n), part(3, h, n), ACT.Square).then_inc(a, 1)
                        for h, o, n in hs:
                            after(tt, ta, 2, "var", h)
                            nc.scalar.activation(part(1, h, n), bank[6 + h][:, 0:n], ACT.Sqrt, bias=eps[:, 0:1]).then_inc(a, 1)
                        for h, o, n in hs:
                            after(v, va, 0, "out", h)
                            nc.scalar.activation(X[:, col(h)], part(5, h, n), ACT.Copy).then_inc(a, 1)
                    if p == BASIS:
                        for h, o, n in hs:
                            after(v, va, 0, "out", h)
                            act.dma_start(outT[:, col(h)], part(5, h, n)).then_inc(out_stored[h], 16)
                    if p in ROWS:
                        view = next_table[p].rearrange("(t p) c -> p t c", p=P)
                        for h, o, n in hs:
                            rows = stage[h][:, 0:n]
                            act.wait_ge(s["rows_ready", h], i + 1)
                            act.wait_ge(s["rows_stored", h], i * 16)
                            nc.scalar.activation(rows, bank[h][:, 0:n], ACT.Copy).then_inc(s["rows_copied", h], 1)
                            act.wait_ge(s["rows_copied", h], i + 1)
                            act.dma_start(view[:, bass.ds(rows0 + o // P, n // P), :],
                                          rows.rearrange("p (t c) -> p t c", c=D)).then_inc(s["rows_stored", h], 16)
                    if p in WIDE:
                        view = next_table[p].rearrange("(t p r) c -> p t (r c)", p=P, r=NREL)

                        def store(k):
                            act.wait_ge(s["lo_taken"], rows0 + (k + 1))
                            act.wait_ge(s["hi_taken"], rows0 + (k + 1))
                            b, _ = slot(i, k, *place)
                            act.dma_start(view[:, bass.ds(rows0 + k, 1), :],
                                          stage[b].unsqueeze(1)).then_inc(s["wide_stored", b], 16)
                        for k in range(tails):
                            act.wait_ge(s["lo_ready"], rows0 + (k + 1))
                            b, stored = slot(i, k, *place)
                            act.wait_ge(s["wide_stored", b], stored)
                            nc.scalar.activation(stage[b][:, 0:512], bank[0][:], ACT.Copy).then_inc(s["lo_taken"], 1)
                            if k:
                                store(k - 1)
                        store(tails - 1)
                if p == GAT:
                    act.wait_ge(acc_zeroed, 1)
                    edge_pass(act, p, needed, off, turn, (node,))
                else:
                    with act.Fori(0, FULL) as j:
                        node(j, None)
                    for n_tile in TAIL_TILES:
                        node(n_tile[0], None, *n_tile[1:])

        @block.tensor
        def _(pe):
            pe.wait_ge(loaded, 16 * NLOAD)
            pe.matmul(bank[0][:, 0:1], mat("WT"), a_sb[:, 0:1], start=True, stop=True)
            pe.matmul(bank[0][:, 1:2], mat("WrT"), a_sb[:, 1:2], start=True, stop=True)
            pe.matmul(bank[0][:, 2:3], mat("WT"), a_sb[:, 2:3], start=True, stop=True).then_inc(t0, 1)
            pe.wait_ge(v0, V0["u2b"])
            pe.matmul(bank[1][:, 0:64], u2b[:], relT_sb[:], start=True, stop=True).then_inc(t0, 1)
            for n in range(NP // P):
                m = pe.matmul(bank[4][:, n:n + 1], X[:, n * P:(n + 1) * P], vv[:, 0:1], start=True, stop=True)
            m.then_inc(t0, 1)

            def q_in(i, *place):
                hs, first, _, _ = tile(i, *place, turn=BIG_TURN)
                for h, o, n in hs:
                    pe.wait_ge(a0, i * 2)
                    pe.matmul(bank[2 + h][:, 0:n], v3b[:], X[:, bass.ds(first + o, n)],
                              start=True, stop=True).then_inc(t0, 1)
            if BIG_FULL:
                with pe.Fori(0, BIG_FULL) as i:
                    q_in(i)
            for n_tile in BIG_TAIL_TILES:
                q_in(*n_tile)
            needed, off = sweeping(pe)
            pe.wait_ge(a0, 2 * (BIG_FULL + 2))
            for p in range(6):
                s = S[p]
                v, a, tt = s["vn"], s["an"], s["tn"]
                part = temporaries(p)
                KV, KA, KT = (n_steps(p, e) for e in range(3))

                placed = [None]

                def turn(T, t, _):
                    for k in range(2):
                        if p == GAT:
                            pe.wait_ge(gmax_part, t * 2 + (k + 1))
                            pe.matmul(bank[2][0:1, 0:P], gm[:, k:k + 1], ident[:], start=True, stop=True).then_inc(gmax_t, 1)
                            pe.wait_ge(gmax_row, t * 2 + (k + 1))
                            pe.matmul(bank[3][:, 0:1], ones[0:1, :], gx[0:1, k:k + 1], start=True, stop=True).then_inc(gmax_all, 1)
                        pe.wait_ge(s["weights_ready", k], t + 1)
                        pe.wait_ge(gathering, (off + NB) * (2 * p) + t * 2 + (k + 1))
                        pe.sem_inc(waited, 1)
                        pe.wait_ge(landed[k], T * (16 * G) + 16 * G)
                        pe.wait_ge(s["taken", k], t)
                        for q in range(GQ):
                            o = bank[k][:, q * 2 * W:(q + 1) * 2 * W]
                            for c in range(q * QUAD, (q + 1) * QUAD):
                                st = dict(start=c % QUAD == 0, stop=c % QUAD == QUAD - 1)
                                if p == BASIS:
                                    m = pe.matmul(o.rearrange("p (a w) -> p a w", a=2), msgs[k][:, c, 0:D], wo[k][:, :, c, :], **st)
                                else:
                                    m = pe.matmul(o[:, 0:W], msgs[k][:, c, 0:D], wo[k][:, 0, c, :], **st)
                            for c in range(q * QUAD, (q + 1) * QUAD):
                                st = dict(start=c % QUAD == 0, stop=c % QUAD == QUAD - 1)
                                if p == GAT:
                                    m = pe.matmul(o[0:1, W:2 * W], ones[:, 0:1], wo[k][:, 0, c, :], **st)
                                if p == GIN1:
                                    m = pe.matmul(o[0:NREL, W:2 * W], oe[k][:, c, :], wo[k][:, 0, c, :], **st)
                        m.then_inc(s["chunk_done", k], 1)
                        if p == GIN2:
                            pe.wait_ge(s["setup"], placed[0])
                            pe.sem_inc(waited, 1)
                            first = windows(pe, T * 2 + k)
                            pe.wait_ge(types_hot, t * 2 + (k + 1))
                            pe.wait_ge(pick_taken, t * 2 + k)
                            for c in range(G):
                                m = pe.matmul(bank[4 + c // 8][:, (c % 8) * W:(c % 8 + 1) * W],
                                              types_b[:, c * P:(c + 1) * P], counts[:, bass.ds(first[c // QUAD], W)],
                                              start=True, stop=True)
                            m.then_inc(picked, 1)

                def node(i, t, *place):
                    hs, first, rows0, tails = tile(i, *place, turn=BIG_TURN if p == GAT else TURN)
                    va, aa, ta = pe.snap(i * KV), pe.snap(i * KA), pe.snap(i * KT)
                    for k in range(2):
                        pe.wait_ge(s["taken", k], t)
                    if p in EXTRA:
                        pe.wait_ge(s["sums"], t * (2 * SUMS[p]))

                    def after(sm, base, e, name, h):
                        pe.wait_ge(sm, base + step_at(p, e, name, h))

                    def col(h):
                        return bass.ds(first + hs[h][1], hs[h][2])
                    pe.wait_ge(v, va)
                    pe.wait_ge(a, aa)
                    if p == GAT:
                        for h, o, n in hs:
                            pe.matmul(bank[6 + h][:, 0:n], ones[0:1, :], acc[0:1, 1, col(h)], start=True, stop=True).then_inc(tt, 1)
                    if p == GIN1:
                        for h, o, n in hs:
                            pe.matmul(bank[6 + h][0:SETS, 0:n], spread[0:NREL, :], acc[0:NREL, 1, col(h)],
                                      start=True, stop=True).then_inc(tt, 1)
                    for h, o, n in hs:
                        out = bank[2 + h][:, 0:n]
                        if p == GAT:
                            after(v, va, 0, "norm", h)
                            pe.matmul(out, mat("W"), part(0, h, n), start=True, stop=True).then_inc(tt, 1)
                        if p in (GIN1, GIN2):
                            after(v, va, 0, "zin", h)
                            pe.matmul(out, mat("W1a" if p == GIN1 else "W2a"), part(0, h, n), start=True, stop=True).then_inc(tt, 1)
                        if p == RGCN1:
                            pe.matmul(out, mat("root0"), X[:, col(h)], start=True, stop=True).then_inc(tt, 1)
                        if p == RGCN2:
                            pe.matmul(out, mat("root1"), H[:, col(h)], start=True, stop=True).then_inc(tt, 1)
                        if p == BASIS:
                            pe.matmul(out, mat("V0"), X[:, col(h)], start=True, stop=False)
                            pe.matmul(out, mat("V1"), acc[:, 0, col(h)], start=False, stop=False)
                            pe.matmul(out, mat("V2"), acc[:, 1, col(h)], start=False, stop=False)
                            pe.matmul(out, mat("loop"), X[:, col(h)], start=False, stop=True).then_inc(tt, 1)
                    if p in (GIN1, GIN2):
                        for h, o, n in hs:
                            after(a, aa, 1, "hidden", h)
                            pe.matmul(bank[4 + h][:, 0:n], mat("W1b" if p == GIN1 else "W2b"), part(1, h, n),
                                      start=True, stop=True).then_inc(tt, 1)
                    if p in NORMED:
                        for h, o, n in hs:
                            after(v, va, 0, "sum", h)
                            mb = 2 if p == GIN2 else 4
                            pe.matmul(bank[mb + h][:, 0:n], mean_m[:], part(2, h, n), start=True, stop=True).then_inc(tt, 1)
                        for h, o, n in hs:
                            after(a, aa, 1, "square", h)
                            pe.matmul(bank[6 + h][:, 0:n], mean_m[:], part(4, h, n), start=True, stop=True).then_inc(tt, 1)

                def node_end(i, t, *place):
                    hs, first, rows0, tails = tile(i, *place, turn=BIG_TURN if p == GAT else TURN)
                    va, aa = pe.snap(i * KV), pe.snap(i * KA)
                    for k in range(2):
                        pe.wait_ge(s["taken", k], t)
                    pe.sem_inc(waited, 1)

                    def after(sm, base, e, name, h):
                        pe.wait_ge(sm, base + step_at(p, e, name, h))

                    def after_out(h):
                        if p in NORMED:
                            after(v, va, 0, "out", h)
                        else:
                            after(a, aa, 1, "outr", h)
                    if p in ROWS:
                        for h, o, n in hs:
                            after_out(h)
                            pe.wait_ge(s["rows_copied", h], i)
                            for k in range(n // P):
                                m = pe.transpose(bank[h][:, k * P:(k + 1) * P], part(5, h, n)[:, k * P:(k + 1) * P], ident[:])
                            m.then_inc(s["rows_ready", h], 1)
                    if p in WIDE:
                        for k in range(tails):
                            h = int(k * P >= hs[1][1])
                            if k * P == hs[h][1]:
                                after_out(h)
                            node = part(5, h, hs[h][2])[:, k * P - hs[h][1]:(k + 1) * P - hs[h][1]]
                            pe.wait_ge(s["lo_taken"], rows0 + k)
                            pe.matmul(bank[0][:], node, tw[:, 0:512], start=True, stop=True).then_inc(s["lo_ready"], 1)
                            pe.wait_ge(s["hi_taken"], rows0 + k)
                            pe.matmul(bank[1][:], node, tw[:, 512:1024], start=True, stop=True).then_inc(s["hi_ready"], 1)
                    if p in ROWS:
                        for h, o, n in hs:
                            pe.wait_ge(s["rows_copied", h], i + 1)
                    if p in WIDE:
                        pe.wait_ge(s["lo_taken"], rows0 + tails)
                        pe.wait_ge(s["hi_taken"], rows0 + tails)
                if p == RGCN1:
                    pe.wait_ge(tw_loaded, 16)

                def sweep_placed(sw):
                    placed[0] = pe.snap((sw + 1) * SETUP[p])

                def pass_placed():
                    placed[0] = pe.snap(needed * ((NSW + 1) * SETUP[p]))

                def inverted():
                    pe.wait_ge(den_moved, 64)
                    pe.sem_inc(waited, 1)
                edge_pass(pe, p, needed, off, turn, (node, node_end), setup=sweep_placed, main=pass_placed,
                          between=inverted)
                pe.wait_ge(v, KV * TILES[p])
                pe.wait_ge(a, KA * TILES[p])

        @block.vector
        def _(dve):
            vec = nc.vector

            def tick0(ins, name):
                ins.then_inc(v0, 1)
                dve.wait_ge(v0, V0[name])
            dve.wait_ge(consts, 2)
            tick0(vec.tensor_copy(iota[:], iota_i[:]), "iota")
            tick0(vec.tensor_copy(pidx[:], pidx_i[:]), "pidx")
            tick0(vec.tensor_scalar(ident[:], iota[:], pidx[:, 0:1], None, ALU.is_equal), "ident")
            tick0(vec.memset(ones[:], 1.0), "ones")
            tick0(vec.memset(mean_m[:], 1.0 / D), "mean")
            tick0(vec.tensor_scalar(in_set[:], pidx[:], 32.0, -32.0, ALU.is_ge, ALU.mult), "set1")
            tick0(vec.tensor_tensor(pidx[:], pidx[:], in_set[:], ALU.add), "set2")
            tick0(vec.tensor_scalar(in_set[:], pidx[:], 32.0, -32.0, ALU.is_ge, ALU.mult), "set3")
            tick0(vec.tensor_tensor(in_set[:], pidx[:], in_set[:], ALU.add), "set4")
            tick0(vec.memset(spread[:], 0.0), "spread0")
            for n, c in enumerate((0, 32, 64)):
                tick0(vec.tensor_copy(spread[:, c:c + NREL], ident[0:NREL, 0:NREL]), f"spread{n + 1}")
            vec.memset(acc[:].rearrange("p a n -> p (a n)"), 0.0).then_inc(acc_zeroed, 1)
            dve.wait_ge(loaded, 16 * NLOAD)
            dq = work[0:QP, 0:2 * QUAD * P].bitcast(I32).rearrange("p (k e) -> p k e", k=2)
            dm = work[0:QP, 2 * QUAD * P:4 * QUAD * P].rearrange("p (k e) -> p k e", k=2)
            tick0(vec.tensor_reduce(bq[:], dq, AX.X, ALU.min), "qmin")
            tick0(vec.tensor_scalar(bq[:], bq[:], float(NP - W), None, ALU.min), "qcl")
            tick0(vec.scalar_tensor_tensor(dm, dq, float(NP), dq, ALU.is_lt, ALU.mult), "qmsk")
            tick0(vec.tensor_reduce(mq[:], dm, AX.X, ALU.max), "qmax")
            tick0(vec.tensor_tensor(mq[:], mq[:], bq[:], ALU.subtract), "qspan")
            tick0(vec.tensor_reduce(wq[:], mq[:], AX.X, ALU.max), "qwide")
            dve.wait_ge(t0, T0["vv"])
            tick0(vec.tensor_copy(vv[:], bank[0][:, 0:3]), "vv")
            tick0(vec.tensor_scalar(v3b[:], ones[:], vv[:, 2:3], None, ALU.mult), "v3b")
            tick0(vec.tensor_scalar(u2b[:], ones[:], vv[:, 1:2], None, ALU.mult), "u2b")
            dve.wait_ge(based_back, 32)
            tick0(vec.tensor_reduce(chk[:, 0:1], wide[:], AX.X, ALU.max), "spans")
            tick0(vec.tensor_scalar(chk[:, 0:1], chk[:, 0:1], float(W), None, ALU.is_ge), "wide")
            for j in range(NT - 1):
                turns, end = (LAG + j * C + 1, (j + 1) * TURN) if j < FULL else (NB - 1, NP - last)
                tick0(vec.tensor_reduce(chk[:, j + 1:j + 2], base_keep[:, turns * QT:], AX.X, ALU.min), f"late{j}a")
                tick0(vec.tensor_scalar(chk[:, j + 1:j + 2], chk[:, j + 1:j + 2], float(end), None, ALU.is_lt), f"late{j}b")
            tick0(vec.tensor_reduce(flag[:, 0:1], chk[:], AX.X, ALU.max), "flag")
            tick0(vec.tensor_scalar(flag[:, 1:2], flag[:, 0:1], -1.0e6, None, ALU.mult), "far")
            tick0(vec.tensor_scalar(flag[:, 2:3], flag[:, 0:1], -1.0, 1.0, ALU.mult, ALU.add), "keepf")
            tick0(vec.tensor_scalar(base_keep[:], base_keep[:], flag[:, 2:3], None, ALU.mult), "base_keep")
            tick0(vec.tensor_copy(flag_i[:], flag[0:1, 0:1]), "flag_i")
            dve.wait_ge(t0, T0["c64"])
            tick0(vec.tensor_copy(c64[:], bank[1][:, 0:64]), "c64")
            dve.wait_ge(t0, T0["pcol"])
            tick0(vec.tensor_copy(pcol[:], bank[4][:, 0:NP // P]), "pcol")

            def place(col, done, gat):
                done(vec.tensor_copy(base_i[:], base_keep[0:1, :]) if col == 1 else
                     vec.tensor_scalar(base_i[:], base_keep[0:1, :], flag[0:1, col:col + 1], None, ALU.add), "base_i")
                done(vec.tensor_scalar(base_f[:], base_keep[:], flag[:, col:col + 1], None, ALU.add), "base_f")
                done(vec.tensor_tensor(rel[:].rearrange("p (q c) -> p q c", c=QUAD),
                                       dst_i[:].rearrange("p (q c) -> p q c", c=QUAD),
                                       base_f[:].unsqueeze(2).broadcast_to([P, NQ, QUAD]), ALU.subtract), "rel")
                if gat:
                    done(vec.tensor_scalar(neg[:], rel[:], 0.0, None, ALU.is_ge), "neg1")
                    done(vec.scalar_tensor_tensor(w_edge[:], rel[:], float(W), neg[:], ALU.is_lt, ALU.mult), "neg2")
                    done(vec.tensor_scalar(neg[:], w_edge[:], 1.0, None, ALU.subtract), "neg3")
                    done(vec.tensor_scalar(neg[:], neg[:], BIG, None, ALU.mult), "neg4")
            place(1, tick0, True)
            tick0(vec.memset(flag[:, 3:4], 0.0), "off")
            tick0(vec.memset(Rmax[:], LOWEST), "R")
            tick0(vec.memset(eps[:], 1e-5), "eps")
            dve.wait_ge(acc_zeroed, 1)
            needed, off = sweeping(dve)
            dve.wait_ge(a0, 2 * (BIG_FULL + 2))

            def over_w(ap):
                return ap.unsqueeze(2).broadcast_to([P, G, W])
            iota_w = iota[:, 0:W].unsqueeze(1).broadcast_to([P, G, W])
            n_pre = 0
            for p in range(6):
                s = S[p]
                chain = s["chain"]

                def pre(ins):
                    nonlocal n_pre
                    ins.then_inc(prep, 1)
                    n_pre += 1
                    dve.wait_ge(prep, n_pre)

                def coefficients(b, dst, scratch):
                    for r in range(NREL):
                        cf = coef[:, 2 * r + b:2 * r + b + 1]
                        if r == 0:
                            pre(vec.tensor_scalar(dst[:], et8_i[:], float(r), cf, ALU.is_equal, ALU.mult))
                        else:
                            pre(vec.tensor_scalar(scratch[:], et8_i[:], float(r), cf, ALU.is_equal, ALU.mult))
                            pre(vec.tensor_tensor(dst[:], dst[:], scratch[:], ALU.add))
                if p:
                    dve.wait_ge(S[p - 1]["vn"], n_steps(p - 1, 0) * TILES[p - 1])
                if p == GIN1:
                    pre(vec.tensor_scalar(row_i[:], src_i[:], float(NREL), None, ALU.mult))
                    vec.tensor_tensor(row_i[:], row_i[:], et8_i[:], ALU.add).then_inc(rows_made, 1)
                if p == GIN2:
                    pre(vec.memset(w_edge[:], 0.0))
                    vec.memset(types.bitcast(F32), 0.0).then_inc(rows_made, 1)
                if p == RGCN1:
                    pre(vec.tensor_scalar(w_edge[:], w_edge[:], 1.0, None, ALU.max))
                    pre(vec.reciprocal(w_edge[:], w_edge[:]))
                    pre(vec.memset(acc[:, 1, :], 0.0))
                if p == RGCN2:
                    coefficients(1, w_edge2, part_edges)
                if p == BASIS:
                    coefficients(0, w_edge, part_edges)

                def setup(sw):
                    base = dve.snap(sw * SETUP[p])
                    n = [0]

                    def done(ins, _):
                        ins.then_inc(s["setup"], 1)
                        n[0] += 1
                        dve.wait_ge(s["setup"], base + n[0])
                    place(3, done, p == GAT)
                    vec.tensor_scalar(flag[:, 3:4], flag[:, 3:4], float(W), None, ALU.add).then_inc(s["setup"], 1)
                    assert n[0] + 1 == SETUP[p]

                def restore():
                    n = [NSW * SETUP[p]]

                    def done(ins, _):
                        ins.then_inc(s["setup"], 1)
                        n[0] += 1
                        dve.wait_ge(s["setup"], n[0])
                    place(1, done, p == GAT)
                    done(vec.memset(flag[:, 3:4], 0.0), "")
                    assert n[0] == (NSW + 1) * SETUP[p]

                def add_group(k, T, t):
                    base = dve.snap((t * 2 + k) * SUMS[p])
                    f = windows(dve, T * 2 + k)
                    dve.wait_ge(s["chunk_done", k], t + 1)
                    if p == GAT:
                        dve.wait_ge(rescaled[k], t + 1)
                    n = 0
                    for q in range(GQ):
                        o = bank[k][:, q * 2 * W:(q + 1) * 2 * W]
                        win = bass.ds(f[q], W)
                        if q == 0:
                            dve.wait_ge(s["taken", 1 - k], t + k)
                        else:
                            dve.wait_ge(s["sums"], base + n)
                        if p in EXTRA:
                            e = EXTRA[p]
                            vec.tensor_tensor(acc[0:e, 1, win], acc[0:e, 1, win], o[0:e, W:2 * W], ALU.add).then_inc(s["sums"], 1)
                            n += 1
                        if p == BASIS:
                            m = vec.tensor_tensor(acc[:, :, win], acc[:, :, win], o.rearrange("p (a w) -> p a w", a=2), ALU.add)
                        else:
                            m = vec.tensor_tensor(acc[:, 0, win], acc[:, 0, win], o[:, 0:W], ALU.add)
                        if q < GQ - 1:
                            m.then_inc(s["sums"], 1)
                            n += 1
                        elif p in EXTRA:
                            m.then_inc(s["taken", k], 1)
                            dve.wait_ge(s["sums"], base + n)
                            dve.sem_inc(waited, 1)
                        else:
                            m.then_inc(s["taken", k], 1)
                    assert n == SUMS[p]

                def turn(T, t, first):
                    chain_base = dve.snap(t * CHAIN[p])
                    n_chain = 0

                    def step(ins):
                        nonlocal n_chain
                        ins.then_inc(chain, 1)
                        n_chain += 1

                    def settle():
                        dve.wait_ge(chain, chain_base + n_chain)
                    for k in range(2):
                        cols = bass.ds(T * (2 * G) + k * G, G)
                        hot = wo[k][:, 0, :, :]
                        f = windows(dve, T * 2 + k) if p == GAT else None
                        dve.wait_ge(s["weights_ready", 1 - k], t + k)
                        if p == GAT:
                            step(vec.tensor_tensor(oh, iota_w, over_w(rel[:, cols]), ALU.is_equal))
                            step(vec.tensor_tensor(logit[:, :, W:W + 64], iota[:, 0:64].unsqueeze(1).broadcast_to([P, G, 64]),
                                                   over_w(et64_i[:, cols]), ALU.is_equal))
                            step(vec.tensor_copy(logit[:, :, W + 64], neg[:, cols]))
                            settle()
                            for q in range(GQ):
                                qs = slice(q * QUAD, (q + 1) * QUAD)
                                step(vec.tensor_tensor(
                                    logit[:, qs, 0:W], oh[:, qs, :],
                                    H[:, bass.ds(f[q], W)].unsqueeze(1).broadcast_to([P, QUAD, W]), ALU.mult))
                            step(vec.tensor_tensor(logit[:, :, W:W + 64], logit[:, :, W:W + 64],
                                                   c64[:].unsqueeze(1).broadcast_to([P, G, 64]), ALU.mult))
                            settle()
                            step(vec.tensor_reduce(s_q[:], logit[:, :, 0:W + 65], AX.X, ALU.add))
                            settle()
                            dve.wait_ge(gathering, t * 2 + (k + 1))
                            dve.sem_inc(waited, 1)
                            dve.wait_ge(landed[k], T * (16 * G) + 16 * G)
                            step(vec.tensor_tensor(att[:, k, :], s_q[:], msgs[k][:, :, D], ALU.add))
                            settle()
                            step(vec.scalar_tensor_tensor(att[:, k, :], att[:, k, :], 0.2, att[:, k, :], ALU.mult, ALU.max))
                            settle()
                            vec.tensor_reduce(gm[:, k:k + 1], att[:, k, :], AX.X, ALU.max).then_inc(gmax_part, 1)
                            dve.wait_ge(gmax_t, t * 2 + (k + 1))
                            vec.tensor_reduce(gx[0:1, k:k + 1], bank[2][0:1, 0:P], AX.X, ALU.max).then_inc(gmax_row, 1)
                            dve.wait_ge(gmax_all, t * 2 + (k + 1))
                            step(vec.tensor_tensor(Rmax[:, k:k + 1], Rmax[:, 1 - k:2 - k], bank[3][:, 0:1], ALU.max))
                            settle()
                            vec.tensor_scalar(nR[:, k:k + 1], Rmax[:, k:k + 1], -1.0, None, ALU.mult).then_inc(shift_ready, 1)
                            vec.tensor_tensor(dR[:, k:k + 1], Rmax[:, 1 - k:2 - k], Rmax[:, k:k + 1], ALU.subtract).then_inc(shift_ready, 1)
                            vec.tensor_tensor(rose[0:1, k:k + 1], Rmax[0:1, 1 - k:2 - k], Rmax[0:1, k:k + 1], ALU.is_lt).then_inc(shift_ready, 1)
                            dve.wait_ge(exp_ready, t * 4 + (2 * k + 2))
                            vec.tensor_tensor(hot, oh, over_w(ex[:, k, :]), ALU.mult).then_inc(s["weights_ready", k], 1)
                            if k == 1:
                                add_group(0, T, t)
                            elif not first:
                                add_group(1, T - 1, t - 1)
                        if p == GIN1:
                            step(vec.tensor_tensor(oe[k][:], iota[:, 0:NREL].unsqueeze(1).broadcast_to([P, G, NREL]),
                                                   et8_i[:, cols].unsqueeze(2).broadcast_to([P, G, NREL]), ALU.is_equal))
                            settle()
                            vec.tensor_tensor(hot, iota_w, over_w(rel[:, cols]), ALU.is_equal).then_inc(s["weights_ready", k], 1)
                        if p == GIN2:
                            vec.tensor_tensor(hot, iota_w, over_w(rel[:, cols]), ALU.is_equal).then_inc(s["weights_ready", k], 1)
                        if p in (RGCN1, RGCN2):
                            step(vec.tensor_tensor(oh, iota_w, over_w(rel[:, cols]), ALU.is_equal))
                            settle()
                            vec.tensor_tensor(hot, oh, over_w(w_edge[:, cols]), ALU.mult).then_inc(s["weights_ready", k], 1)
                        if p == BASIS:
                            step(vec.tensor_tensor(oh, iota_w, over_w(rel[:, cols]), ALU.is_equal))
                            settle()
                            step(vec.tensor_tensor(hot, oh, over_w(w_edge[:, cols]), ALU.mult))
                            settle()
                            vec.tensor_tensor(wo[k][:, 1, :, :], oh, over_w(w_edge2[:, cols]), ALU.mult).then_inc(s["weights_ready", k], 1)
                    if p != GAT:
                        for k in range(2):
                            if p == GIN2:
                                dve.wait_ge(types_loaded, t * 96 + (48 * (k + 1)))
                                dve.wait_ge(picked, t * 2 + k)
                                vec.tensor_scalar(types_b, types, in_set[0:SETS, 0:1], None, ALU.is_equal).then_inc(types_hot, 1)
                            add_group(k, T, t)
                            if p == GIN2:
                                dve.wait_ge(picked, t * 2 + (k + 1))
                                own = wo[k][:, 0, :, :]
                                step(vec.tensor_tensor(tmp[:, 0:8, :], own[:, 0:8, :],
                                                       bank[4][:].rearrange("p (g w) -> p g w", g=8), ALU.mult))
                                vec.tensor_tensor(tmp[:, 8:16, :], own[:, 8:16, :],
                                                  bank[5][:].rearrange("p (g w) -> p g w", g=8), ALU.mult).then_inc(pick_taken, 1)
                                settle()
                                dve.wait_ge(pick_taken, t * 2 + (k + 1))
                                step(vec.tensor_reduce(s_q[:], tmp, AX.X, ALU.add))
                                settle()
                                cols = bass.ds(T * (2 * G) + k * G, G)
                                step(vec.tensor_tensor(w_edge[:, cols], w_edge[:, cols], s_q[:], ALU.add))
                    assert n_chain == CHAIN[p], (p, n_chain, CHAIN[p])

                def flush(T, t):
                    add_group(1, T, t)
                v, a, tt = s["vn"], s["an"], s["tn"]
                part = temporaries(p)
                KV, KA, KT = (n_steps(p, e) for e in range(3))

                def node(i, t, *place):
                    hs, first, rows0, tails = tile(i, *place, turn=BIG_TURN if p == GAT else TURN)
                    va, aa, ta = dve.snap(i * KV), dve.snap(i * KA), dve.snap(i * KT)
                    dve.wait_ge(s["taken", 1], t)

                    def after(sm, base, e, name, h):
                        dve.wait_ge(sm, base + step_at(p, e, name, h))

                    def col(h):
                        return bass.ds(first + hs[h][1], hs[h][2])
                    if p == GAT:
                        for h, o, n in hs:
                            after(tt, ta, 2, "den", h)
                            dve.wait_ge(a, aa)
                            vec.tensor_tensor(part(0, h, n), acc[:, 0, col(h)], bank[6 + h][:, 0:n], ALU.mult).then_inc(v, 1)
                        for h, o, n in hs:
                            after(tt, ta, 2, "lin", h)
                            vec.tensor_tensor(part(2, h, n), bank[2 + h][:, 0:n], X[:, col(h)], ALU.add).then_inc(v, 1)
                    if p in (GIN1, GIN2):
                        for h, o, n in hs:
                            dve.wait_ge(tt, ta)
                            dve.wait_ge(a, aa)
                            vec.tensor_tensor(part(0, h, n), acc[:, 0, col(h)], (X if p == GIN1 else H)[:, col(h)], ALU.add).then_inc(v, 1)
                    if p == GIN1:
                        for h, o, n in hs:
                            after(tt, ta, 2, "counts", h)
                            vec.tensor_copy(counts[:, col(h)], bank[6 + h][0:SETS, 0:n]).then_inc(v, 1)
                        for h, o, n in hs:
                            after(v, va, 0, "hi", h)
                            vec.tensor_tensor(part(2, h, n)[0:SETS], bank[6 + h][0:SETS, 0:n], counts[:, col(h)], ALU.subtract).then_inc(v, 1)
                        for h, o, n in hs:
                            after(v, va, 0, "rest", h)
                            vec.tensor_copy(part(3, h, n)[0:SETS].bitcast(BF16)[:, 0:n], part(2, h, n)[0:SETS]).then_inc(v, 1)
                        for h, o, n in hs:
                            after(v, va, 0, "mid", h)
                            vec.tensor_tensor(part(2, h, n)[0:SETS], part(2, h, n)[0:SETS], part(3, h, n)[0:SETS].bitcast(BF16)[:, 0:n],
                                              ALU.subtract).then_inc(v, 1)
                        for h, o, n in hs:
                            after(v, va, 0, "low", h)
                            vec.tensor_copy(counts[32:32 + NREL, col(h)], part(3, h, n)[32:32 + NREL].bitcast(BF16)[:, 0:n]).then_inc(v, 1)
                        for h, o, n in hs:
                            vec.tensor_copy(counts[64:64 + NREL, col(h)], part(2, h, n)[64:64 + NREL]).then_inc(v, 1)
                        for h, o, n in hs:
                            after(a, aa, 1, "outr", h)
                            vec.tensor_copy(H[:, col(h)], part(5, h, n)).then_inc(v, 1)
                    if p == GIN2:
                        for h, o, n in hs:
                            after(tt, ta, 2, "lin2", h)
                            vec.scalar_tensor_tensor(part(2, h, n), bank[4 + h][:, 0:n], bcol("b2b"), X[:, col(h)],
                                                     ALU.add, ALU.add).then_inc(v, 1)
                    if p == RGCN1:
                        for h, o, n in hs:
                            after(tt, ta, 2, "lin", h)
                            dve.wait_ge(a, aa)
                            vec.tensor_tensor(part(2, h, n), bank[2 + h][:, 0:n], acc[:, 0, col(h)], ALU.add).then_inc(v, 1)
                        for h, o, n in hs:
                            after(a, aa, 1, "outr", h)
                            vec.tensor_copy(H[:, col(h)], part(5, h, n)).then_inc(v, 1)
                    if p == RGCN2:
                        for h, o, n in hs:
                            after(tt, ta, 2, "lin", h)
                            vec.tensor_tensor(part(0, h, n), bank[2 + h][:, 0:n], acc[:, 0, col(h)], ALU.add).then_inc(v, 1)
                        for h, o, n in hs:
                            after(v, va, 0, "sum0", h)
                            vec.scalar_tensor_tensor(part(2, h, n), part(0, h, n), bcol("bias1"), X[:, col(h)], ALU.add, ALU.add).then_inc(v, 1)
                    if p == BASIS:
                        for h, o, n in hs:
                            after(tt, ta, 2, "lin", h)
                            vec.scalar_tensor_tensor(part(2, h, n), bank[2 + h][:, 0:n], bcol("h_bias"), X[:, col(h)],
                                                     ALU.add, ALU.add).then_inc(v, 1)
                    if p in NORMED:
                        mb = 2 if p == GIN2 else 4
                        for h, o, n in hs:
                            after(tt, ta, 2, "mean", h)
                            after(v, va, 0, "sum", h)
                            vec.tensor_tensor(part(3, h, n), part(2, h, n), bank[mb + h][:, 0:n], ALU.subtract).then_inc(v, 1)
                        for h, o, n in hs:
                            after(a, aa, 1, "std", h)
                            vec.reciprocal(part(0, h, n), part(1, h, n)).then_inc(v, 1)
                        for h, o, n in hs:
                            after(v, va, 0, "rstd", h)
                            if p in ROWS:
                                dve.wait_ge(s["rows_ready", h], i)
                            if p in WIDE:
                                dve.wait_ge(s["hi_ready"], rows0)
                            if p == BASIS:
                                dve.wait_ge(out_stored[h], i * 16)
                            vec.tensor_tensor(part(5, h, n), part(3, h, n), part(0, h, n), ALU.mult).then_inc(v, 1)
                    dve.wait_ge(v, va + KV - (2 if p != BASIS else 0))

                def node_end(i, t, *place):
                    hs, first, rows0, tails = tile(i, *place, turn=BIG_TURN if p == GAT else TURN)
                    va = dve.snap(i * KV)
                    dve.wait_ge(s["taken", 1], t)
                    dve.sem_inc(waited, 1)

                    def col(h):
                        return bass.ds(first + hs[h][1], hs[h][2])
                    if p != BASIS:
                        both = acc[:] if p == GAT else acc[:, 0:1, :]
                        for h, o, n in hs:
                            block = both[:, :, col(h)]
                            vec.tensor_scalar(block, block, 0.0, None, ALU.mult).then_inc(v, 1)
                    if p in WIDE:
                        for k in range(tails):
                            dve.wait_ge(s["hi_ready"], rows0 + (k + 1))
                            b, stored = slot(i, k, *place)
                            dve.wait_ge(s["wide_stored", b], stored)
                            vec.tensor_copy(stage[b][:, 512:1024], bank[1][:]).then_inc(s["hi_taken"], 1)
                    dve.wait_ge(v, va + KV)

                def invert():
                    dve.wait_ge(den_moved, 32)
                    vec.tensor_scalar(den[:], den[:], 1e-10, None, ALU.add).then_inc(den_inverted, 1)
                    dve.wait_ge(den_inverted, 1)
                    vec.reciprocal(den[:], den[:]).then_inc(den_inverted, 1)
                edge_pass(dve, p, needed, off, turn, (node, node_end), setup, restore, flush if p == GAT else None,
                          between=invert)


INS = ["x_rows", "xT", "src_pt", "dst_pt", "dst_q", "et64_pt", "et8_pt", "et8_flat", "mats", "bias", "avec", "relT",
       "tw0", "tw1", "coeff"]


def lay_out(x, src, dst, edge_type_64, edge_type_8, w):
    N, E = x.shape[0], src.shape[0]
    NP, NCH = sizes(N, E)

    def padded(a, fill):
        return np.concatenate([a, np.full(NCH * P - E, fill, a.dtype)])

    def pt(a):
        return np.ascontiguousarray(a.reshape(NCH, P).T)
    d, e8 = padded(dst, 4 * NP), padded(edge_type_8, 0)
    return {
        "x_rows": np.concatenate([x, np.zeros((NP - N, D), x.dtype)]),
        "xT": np.ascontiguousarray(np.concatenate([x, np.zeros((NP - N, D), x.dtype)]).T),
        "src_pt": pt(padded(src, 0)), "dst_pt": pt(d), "dst_q": d.reshape(NCH // QUAD // 2, 2 * QUAD * P),
        "et64_pt": pt(padded(edge_type_64, 0)), "et8_pt": pt(e8), "et8_flat": e8.reshape(1, -1),
        "mats": np.concatenate([w["L0_gnn_W"], w["L1_gnn_W1a"], w["L1_gnn_W1b"], w["L1_gnn_W2a"], w["L1_gnn_W2b"],
                                w["L2_gnn_roots"][0], w["L2_gnn_roots"][1], w["L3_gnn_W"][0], w["L3_gnn_W"][1],
                                w["L3_gnn_W"][2], w["L3_gnn_loop_weight"], w["L0_gnn_W"].T, w["L0_gnn_W_r"].T], axis=1),
        "bias": np.stack([w["L1_gnn_b1a"], w["L1_gnn_b1b"], w["L1_gnn_b2a"], w["L1_gnn_b2b"], w["L2_gnn_biases"][0],
                          w["L2_gnn_biases"][1], w["L3_gnn_h_bias"]], axis=1),
        "avec": np.ascontiguousarray(w["L0_gnn_a"].reshape(3, D).T),
        "relT": np.ascontiguousarray(w["L0_gnn_rel_emb"].T),
        "tw0": np.concatenate(list(w["L2_gnn_weights"][0]), axis=1),
        "tw1": np.concatenate(list(w["L2_gnn_weights"][1]), axis=1),
        "coeff": np.ascontiguousarray(w["L3_gnn_coeff"].reshape(1, -1)),
    }


def kernel(x, src, dst, edge_type_64, edge_type_8, **weights):
    import concourse.bacc as bacc
    from concourse.bass_utils import run_bass_kernel_spmd

    x, src, dst, e64, e8 = (np.asarray(a) for a in (x, src, dst, edge_type_64, edge_type_8))
    N, E = x.shape[0], src.shape[0]
    arrays = lay_out(x, src, dst, e64, e8, {k: np.asarray(v) for k, v in weights.items()})
    nc = bacc.Bacc("TRN2", target_bir_lowering=False, num_devices=1)
    args = [nc.dram_tensor(n, arrays[n].shape, mybir.dt.from_np(arrays[n].dtype), kind="ExternalInput").ap() for n in INS]
    outT = nc.dram_tensor("outT", [P, sizes(N, E)[0]], F32, kind="ExternalOutput").ap()
    with nc.allow_non_contiguous_dma("columns of small arrays"):
        build(nc, N, E, *args, outT)
    r = run_bass_kernel_spmd(nc, [arrays], core_ids=[0])
    return np.ascontiguousarray(r.results[0]["outT"][:, :N].T)
```
